# Optimizing a Trainium2 kernel written in Bass

```python
import numpy as np
import jax
import jax.numpy as jnp

def _softmax(x, axis=-1):
    return jax.nn.softmax(x, axis=axis)

def _gelu(x):
    return jax.nn.gelu(x, approximate=True)

def _silu(x):
    return jax.nn.silu(x)

def _sigmoid(x):
    return jax.nn.sigmoid(x)

def _layernorm(x, axis=-1, eps=1e-05):
    m = jnp.mean(x, axis=axis, keepdims=True)
    v = jnp.var(x, axis=axis, keepdims=True)
    return (x - m) / jnp.sqrt(v + eps)

def _scatter_add(tgt, idx, src, axis=0):
    return tgt.at[idx].add(src)

def _segment_sum(src, seg, n):
    return jax.ops.segment_sum(src, seg, n)
kernel_name = 'mk_adj_resnorm_d2_adj_r2_4be96d'

def setup_inputs(seed: int=0):
    np.random.seed(seed)
    _w = jnp.asarray

    def _rec_inputs():
        import jax
        import jax.numpy as jnp
        _gk = jax.random.key(seed)
        x = -0.0005207 + 1.001 * jax.random.normal(jax.random.fold_in(_gk, 1), (2048, 256), jnp.float32)
        _a = jax.random.bernoulli(jax.random.fold_in(_gk, 2), 0.00195312, (2048, 2048))
        _a = jnp.logical_or(_a, jnp.swapaxes(_a, -1, -2))
        _a = jnp.logical_or(_a, jnp.eye(2048, dtype=bool))
        adj = _a.astype(jnp.int32)
        return (x, adj)
    x, adj = _rec_inputs()

    def _L0_gnn_setup():
        import jax, jax.numpy as jnp
        import numpy as np
        HEAD_SIZE = 8
        QK_DIM = 256
        V_DIM = 256
        N = 2048
        ATT_DIM = QK_DIM // HEAD_SIZE
        SCALE = ATT_DIM ** (-0.5)
        NEG_FILL = jnp.float32(-9000000000000000.0)
        key = jax.random.key(seed)
        k1, k2, k3, k4 = jax.random.split(key, 4)
        x1 = jax.random.normal(k1, (N, QK_DIM), dtype=jnp.float32)
        x2 = jax.random.normal(k2, (N, QK_DIM), dtype=jnp.float32)
        v = jax.random.normal(k3, (N, V_DIM), dtype=jnp.float32)
        adj = jax.random.randint(k4, (N, N), 0, 2, dtype=jnp.int32)
        return {'x1': x1, 'x2': x2, 'v': v, 'adj': adj}
    _L0_gnn_all = _L0_gnn_setup()
    _L0_gnn_in = {k: v for k, v in _L0_gnn_all.items() if k in ('x2', 'v')}
    del _L0_gnn_all

    def _L1_gnn_setup():
        import jax, jax.numpy as jnp
        import numpy as np
        EPS = 1e-08
        key = jax.random.key(seed)
        k1, k2, k3 = jax.random.split(key, 3)
        N, IN_DIM, OUT_DIM = (4096, 256, 256)
        h = jax.random.normal(k1, (N, IN_DIM), dtype=jnp.float32)
        adj = jax.random.randint(k2, (N, N), 0, 2, dtype=jnp.int32)
        W = jax.random.normal(k3, (OUT_DIM, IN_DIM), dtype=jnp.float32) * (1.0 / np.sqrt(IN_DIM))
        return {'h': h, 'adj': adj, 'W': W}
    _L1_gnn_all = _L1_gnn_setup()
    _L1_gnn_in = {k: v for k, v in _L1_gnn_all.items() if k in ('W',)}
    del _L1_gnn_all
    return {'x': x, 'adj': adj, 'L0_gnn_x2': _L0_gnn_in['x2'], 'L0_gnn_v': _L0_gnn_in['v'], 'L1_gnn_W': _L1_gnn_in['W']}

def reference(x, adj, L0_gnn_x2, L0_gnn_v, L1_gnn_W):
    import jax
    import jax.numpy as jnp

    def _L0_gnn_ref(x1, x2, v, adj):
        import jax, jax.numpy as jnp
        import numpy as np
        HEAD_SIZE = 8
        QK_DIM = 256
        V_DIM = 256
        N = 2048
        ATT_DIM = QK_DIM // HEAD_SIZE
        SCALE = ATT_DIM ** (-0.5)
        NEG_FILL = jnp.float32(-9000000000000000.0)
        n = x1.shape[0]
        q = x1.reshape(n, HEAD_SIZE, -1).transpose(1, 0, 2) * SCALE
        k = x2.reshape(n, HEAD_SIZE, -1).transpose(1, 0, 2)
        vv = v.reshape(n, HEAD_SIZE, -1).transpose(1, 0, 2)
        scores = jnp.einsum('hnd,hmd->hnm', q, k)
        scores = jnp.where(adj > 0, scores, NEG_FILL)
        attn = jax.nn.softmax(scores, axis=-1)
        out = jnp.einsum('hnm,hmd->hnd', attn, vv)
        return out.transpose(1, 0, 2).reshape(n, -1)

    def _L1_gnn_ref(h, adj, W):
        import jax, jax.numpy as jnp
        import numpy as np
        EPS = 1e-08
        Wh = h @ W.T
        N = Wh.shape[0]
        norms = jnp.linalg.norm(Wh, axis=1, keepdims=True)
        sim = Wh @ Wh.T / (norms * norms.T + EPS)
        mask = (adj > 0) | jnp.eye(N, dtype=bool)
        sim_masked = jnp.where(mask, sim, -jnp.inf)
        alpha = jax.nn.softmax(sim_masked, axis=1)
        return alpha @ Wh
    x = _layernorm(x + _L0_gnn_ref(x, L0_gnn_x2, L0_gnn_v, adj), axis=-1)
    x = _layernorm(x + _L1_gnn_ref(x, adj, L1_gnn_W), axis=-1)
    return x

_drawn_inputs = setup_inputs


def setup_inputs(seed=0):
    import zlib

    import numpy as np

    out = dict(_drawn_inputs(seed))
    spreads = {}
    factors = {}
    for name, (base, spread) in spreads.items():
        noise = np.random.default_rng([zlib.crc32(name.encode()), seed]).standard_normal(out[name].shape)
        drawn = base * np.exp(spread * noise) if base else spread * noise
        out[name] = jnp.asarray(drawn.astype(out[name].dtype))
    for name, factor in factors.items():
        out[name] = (out[name] * factor).astype(out[name].dtype)
    return out
```

```python
from contextlib import ExitStack

import concourse.bass as bass
from concourse import mybir

F32 = mybir.dt.float32
F32R = mybir.dt.float32r
BF16 = mybir.dt.bfloat16
I32 = mybir.dt.int32
ALU = mybir.AluOpType
ACT = mybir.ActivationFunctionType

P = 128
LN_EPS = 1e-5
COS_EPS = 1e-8
MASKED = -(2.0 ** 53)
HEADS = 8


def build(nc, x, adj, x2, v, W, out):
    N, D = x.shape
    HD = D // HEADS
    SCALE = HD ** -0.5
    NT = N // P
    KT = D // P
    QT = 2
    QB = QT * P
    NB = N // QB
    STEPS = HEADS * NB
    CH = 1024
    NCH = N // CH
    SU = QT * NCH
    JU = 2
    TU = NT // JU
    PVG = 4
    BODY = 2 * NB
    LOOPS = HEADS // 2 - 1
    assert (HD, NT, KT, NB, SU, TU) == (32, 16, 2, 8, 4, 8)

    xt_dram = x.rearrange("(t p) d -> p t d", p=P)
    kt_dram = x2.rearrange("(t p) d -> p t d", p=P)
    vt_dram = v.rearrange("(t p) d -> p t d", p=P)
    adj_dram = adj.rearrange("(t p) m -> t p m", p=P)
    out_dram = out.rearrange("(t p) d -> p t d", p=P)

    def units_of(k):
        u = [("qk", k + 1, 2), ("qk", k + 1, 3)]
        if k % 2 == 0:
            u.append(("fin", k))
        if k % NB in PREP_STEPS:
            u.append(("prep", k))
        u += [("qk", k + 2, 0), ("qk", k + 2, 1)]
        return u
    PREP_STEPS = (2, 3, 4, 5)
    PRE = [("prep", i) for i in range(4)] + [("qk", 0, c) for c in range(SU)] + [("qk", 1, 0), ("qk", 1, 1)]
    PRE += [("qk", 1, 2), ("qk", 1, 3), ("qk", 2, 0), ("qk", 2, 1)]
    BODY_UNITS = [u for k in range(1, BODY + 1) for u in units_of(k)]
    assert len(PRE) % 2 == 0 and len(BODY_UNITS) % 2 == 0
    def exists(u):
        return LOOPS * BODY + u[1] < STEPS if u[0] == "qk" else u[0] == "fin" or u[1] < NB
    LAST_UNITS = [u for u in BODY_UNITS if exists(u) and u != ("fin", BODY)] + [("fin", BODY)]

    def unit(hp, key):
        units = LAST_UNITS if isinstance(hp, int) and hp == LOOPS else BODY_UNITS
        i = units.index(key)
        return i % 2, hp * len(BODY_UNITS) + (len(PRE) + i)

    def mask_unit(hp, kk, c):
        if kk == 2 and c < 2:
            return c, hp * len(BODY_UNITS) + (len(PRE) - 2 + c)
        return unit(hp, ("qk", kk, c))

    def act_share(k):
        return 6 if k % 2 == 0 else 5

    def acts(hp, k, u):
        before = 11 * (k // 2) + 6 * (k % 2)
        return hp * (11 * BODY // 2) + (before + min(u + 1, act_share(k)))

    def dves(hp, k, u):
        before = 5 * (k // 2) + 2 * (k % 2)
        return hp * (5 * BODY // 2) + (before + max(0, u + 1 - act_share(k)))

    with ExitStack() as ctx:
        def sb(name, shape, dt=F32):
            return ctx.enter_context(nc.sbuf_tensor(name, shape, dt))

        def sem(name):
            return ctx.enter_context(nc.semaphore(name))

        score_ps = ctx.enter_context(nc.psum_tensor("score_ps", [P, 2, CH], F32))
        turn_ps = [ctx.enter_context(nc.psum_tensor(f"turn_ps{i}", [P, 512], F32)) for i in range(3)]
        o_ps = ctx.enter_context(nc.psum_tensor("o_ps", [P, 2, QB], F32))

        mask = sb("mask", [P, NT, N], BF16)
        ident = sb("ident", [P, P])
        ones = sb("ones", [P, P])
        attn = sb("attn", [P, NT, D])
        prob = sb("prob", [P, 4, N])
        neg_max = sb("neg_max", [P, 8, 2])
        row_sum = sb("row_sum", [P, 8])
        inv_sum = sb("inv_sum", [P, 4])
        stats = sb("stats", [P, 4, 6])
        mean_var = sb("mean_var", [P, NT, 2])
        rstd = sb("rstd", [P, NT])
        norm_col = sb("norm_col", [P, NT])
        eps = sb("eps", [P, 2])

        with ExitStack() as layer0:
            def sb0(name, shape, dt=F32):
                return layer0.enter_context(nc.sbuf_tensor(name, shape, dt))

            q_hl = [sb0(f"q_hl{b}", [P, N], F32R) for b in range(2)]
            k_hl = [sb0(f"k_hl{b}", [P, N], F32R) for b in range(2)]
            pt = sb0("pt", [P, TU, 2 * QB])
            raw = [[sb0(f"raw_{n}{b}", [P, NT, HD]) for n in "qkv"] for b in range(2)]
            scaled = sb0("scaled", [P, NT, HD])
            parts = [sb0(f"parts{i}", [P, NT // 2, 4, HD], F32R) for i in range(2)]
            o_part = sb0("o_part", [P, 2 * QB])
            w_raw = sb0("w_raw", [P, KT, D])
            wt = sb0("wt", [P, KT, D])
            o_sum = sb0("o_sum", [P, 2 * QT, HD])
            with ExitStack() as masking:
                adj_in = [masking.enter_context(nc.sbuf_tensor(f"adj_in{b}", [P, N], I32)) for b in range(2)]
            x_raw = sb0("x_raw", [P, NT, D])

        w_hl = sb("w_hl", [P, 2, KT, N], F32R)
        wn_hl = sb("wn_hl", [P, 2, NT, D], F32R)
        norm_bc = sb("norm_bc", [P, N])
        e_hl = sb("e_hl", [P, 2, 4, 2 * QB], F32R)
        acc_sb = sb("acc_sb", [P, KT, QB])
        cur = sb("cur", [P, 2, 2, KT, P], F32R)

        raw_in = [sem(f"raw_in{b}") for b in range(2)]
        adj_landed = [sem(f"adj_landed{b}") for b in range(2)]
        mask_made = sem("mask_made")
        const_made = sem("const_made")
        const_step = sem("const_step")
        q_scaled = sem("q_scaled")
        hi_made = sem("hi_made")
        parts_made = sem("parts_made")
        unit_filled = sem("unit_filled")
        unit_emptied = sem("unit_emptied")
        tile_exped = sem("tile_exped")
        turned = sem("turned")
        act_copied = sem("act_copied")
        dve_copied = sem("dve_copied")
        pv_done = sem("pv_done")
        o_taken = sem("o_taken")
        attn_made = sem("attn_made")
        inv_made = sem("inv_made")
        dve_passed = sem("dve_passed")
        pool_passed = sem("pool_passed")
        out_done = sem("out_done")
        x_landed, w_landed = sem("x_landed"), sem("w_landed")
        wt_turned, wt_copied = sem("wt_turned"), sem("wt_copied")
        x_added, stats_made, aggregated = sem("x_added"), sem("stats_made"), sem("aggregated")
        std_made, rstd_made, x1_made = sem("std_made"), sem("rstd_made"), sem("x1_made")
        x1_turned, x1_copied = sem("x1_turned"), sem("x1_copied")
        wh_made, hi_taken, lo_taken, squared = sem("wh_made"), sem("hi_taken"), sem("lo_taken"), sem("squared")
        summed, norm_made, norm_turned, norm_taken = sem("summed"), sem("norm_made"), sem("norm_turned"), sem("norm_taken")
        hi_turned, hi_copied = sem("hi_turned"), sem("hi_copied")
        lo_turned, lo_copied = sem("lo_turned"), sem("lo_copied")
        diagonal_cleared, cur_made = sem("diagonal_cleared"), sem("cur_made")
        sim_filled, sim_emptied = sem("sim_filled"), sem("sim_emptied")
        log_made, inv_norms_made, sim_masked, tile_exped1 = sem("log_made"), sem("inv_norms_made"), sem("sim_masked"), sem("tile_exped1")
        turned1, hi_copied1, lo_copied1, pv1_done, acc_taken = (
            sem("turned1"), sem("hi_copied1"), sem("lo_copied1"), sem("pv1_done"), sem("acc_taken"))
        inv1_made, y_made, var_made, rstd1_log, rstd1_made, out_made = (
            sem("inv1_made"), sem("y_made"), sem("var_made"), sem("rstd1_log"), sem("rstd1_made"), sem("out_made"))

        block = ctx.enter_context(nc.Block())

        def head_cols(hp, k):
            return bass.ds(hp * (2 * HD) + (k // NB) * HD, HD)

        def stand(engine, passed):
            engine.sem_inc(passed, 1)

        CT = 4
        CC = CT * P
        SEAM = ("x0 x1 w0 w1 s0 h0 l0 x2 s1 n0 h1 l1 w2 x3 s2 n1 h2 l2 w3 s3 n2 h3 l3 n3").split()
        SEAM_RING = [u for u in SEAM if u[0] in "xhl"]
        SEAM_FREED = {"x": x1_copied, "h": hi_copied, "l": lo_copied}

        SIM_ORDER = [(0, c) for c in range(SU)] + [(1, 0), (1, 1)] + [(1, 2), (1, 3), (2, 0), (2, 1)]
        for k in range(1, NB):
            SIM_ORDER += [u for u in ((k + 1, 2), (k - 1, "fin"), (k + 1, 3), (k + 2, 0), (k + 2, 1))
                          if u[1] == "fin" or u[0] < NB]
        SIM_ORDER.append((NB - 1, "fin"))
        PAIR = 2

        def sim_unit(j, key):
            i = SIM_ORDER.index(key)
            return i % 2, j * 10 + i

        def rows(j, t, n=1):
            return bass.ds(j * (PAIR * QT) + t, n)

        @block.sync
        def _(sp):
            def load_head(cols, b):
                for dst, src in zip(raw[b], (xt_dram, kt_dram, vt_dram)):
                    sp.dma_start(dst[:], src[:, :, cols]).then_inc(raw_in[b], 16)

            load_head(slice(0, HD), 0)
            for t in range(NT):
                if t >= 2:
                    sp.wait_ge(mask_made, t - 1)
                sp.dma_start(adj_in[t % 2][:], adj_dram[t]).then_inc(adj_landed[t % 2], 16)
                if t == 1:
                    load_head(slice(HD, 2 * HD), 1)
                    sp.dma_start(w_raw[:], W.rearrange("(t p) d -> p t d", p=P)).then_inc(w_landed, 16)

            def next_heads(hp, b):
                sp.wait_ge(pv_done, (hp * 2 + (b + 1)) * (NB * PVG))
                load_head(bass.ds(hp * (2 * HD) + (2 + b) * HD, HD), b)

            sp.wait_ge(mask_made, NT)
            sp.dma_start(x_raw[:], xt_dram).then_inc(x_landed, 16)
            with sp.Fori(0, LOOPS) as hp:
                next_heads(hp, 0)
                next_heads(hp, 1)

            def store(j, k):
                sp.wait_ge(out_made, (j * PAIR + (k + 1)) * QT)
                sp.dma_start(out_dram[:, rows(j, k * QT, QT), :], attn[:, rows(j, k * QT, QT), :]).then_inc(out_done, 16)

            store(0, 0)
            with sp.Fori(0, 2) as j:
                store(j, 1)
                store(j, 2)
            for k in range(5, NB):
                store(0, k)
            sp.wait_ge(out_done, 16 * NB)

        @block.gpsimd
        def _(pool):
            nc.gpsimd.memset(ident[:], 0.0).then_inc(const_step, 1)
            pool.wait_ge(const_step, 1)
            nc.gpsimd.affine_select(out=ident[:], in_=ident[:], compare_op=ALU.not_equal, fill=1.0, base=0,
                                    pattern=[[-1, P]], channel_multiplier=1).then_inc(const_made, 1)

            def split(h, i, b, read):
                half = slice((i % 2) * (NT // 2), (i % 2 + 1) * (NT // 2))
                src = scaled[:, half, :] if i < 2 else raw[b][1][:, half, :]
                hi, lo = ((0, 1), (2, 3)) if i < 2 else ((0, 2), (1, 3))
                dst = parts[i % 2]
                pool.wait_ge(q_scaled, h + 1)
                if read is not None:
                    pool.wait_ge(unit_filled, read)
                stand(pool, pool_passed)
                for r in hi:
                    nc.gpsimd.tensor_scalar(dst[:, :, r, :], src, 1.0, 0.0, ALU.mult, ALU.add).then_inc(hi_made, 1)
                pool.wait_ge(hi_made, h * 8 + (i * 2 + 2))
                for r in lo:
                    nc.gpsimd.tensor_tensor(dst[:, :, r, :], src, dst[:, :, hi[0], :].bitcast(F32),
                                            ALU.subtract).then_inc(parts_made, 1)

            def scale_q(h, b, landed, read):
                pool.wait_ge(raw_in[b], landed)
                if read is not None:
                    pool.wait_ge(parts_made, read)
                stand(pool, pool_passed)
                nc.gpsimd.tensor_scalar(scaled[:], raw[b][0][:], SCALE, 0.0, ALU.mult, ALU.add).then_inc(q_scaled, 1)

            nc.gpsimd.memset(ones[:], 1.0).then_inc(const_made, 1)
            nc.gpsimd.memset(eps[:, 0:1], COS_EPS).then_inc(const_made, 1)
            nc.gpsimd.memset(eps[:, 1:2], LN_EPS).then_inc(const_made, 1)
            scale_q(0, 0, 48, None)
            for i in range(4):
                split(0, i, 0, None if i < 2 else i - 1)
            scale_q(1, 1, 48, None)
            for i in range(4):
                split(1, i, 1, 3 + i if i < 2 else unit(0, ("prep", i))[1] + 1)

            def body(hp):
                scale_q(hp * 2 + 2, 0, hp * 48 + 96, None)
                for i in range(4):
                    split(hp * 2 + 2, i, 0, unit(hp, ("prep", i + 4 if i < 2 else i + 8))[1] + 1)
                scale_q(hp * 2 + 3, 1, hp * 48 + 96, None)
                for i in range(4):
                    split(hp * 2 + 3, i, 1, (unit(hp, ("prep", i + 12)) if i < 2 else unit(hp + 1, ("prep", i)))[1] + 1)
            with pool.Fori(0, LOOPS) as hp:
                body(hp)

            pool.wait_ge(x_landed, 16)
            for c in range(NT // CT):
                pool.wait_ge(attn_made, (HEADS - 1) * (NB // 2) + c + 1)
                nc.gpsimd.tensor_tensor(attn[:, c * CT:(c + 1) * CT, :], attn[:, c * CT:(c + 1) * CT, :],
                                        x_raw[:, c * CT:(c + 1) * CT, :], ALU.add).then_inc(x_added, 1)
            for t in range(NT):
                block_ = mask[:, t, t * P:(t + 1) * P]
                nc.gpsimd.affine_select(out=block_, in_=block_, compare_op=ALU.not_equal, fill=0.0, base=0,
                                        pattern=[[-1, P]], channel_multiplier=1).then_inc(diagonal_cleared, 1)

            def stage(j, t):
                if isinstance(j, int) and j == 0 and t < 2:
                    pool.wait_ge(hi_taken, 2 * (NT // CT))
                    pool.wait_ge(lo_taken, 2 * (NT // CT))
                else:
                    pool.wait_ge(sim_filled, sim_unit(j, ((t - 2) // QT, (t - 2) % QT * NCH + NCH - 1))[1] + 1)
                cols = bass.ds(j * (PAIR * QT * P) + t * P, P)
                for hl in range(2):
                    nc.gpsimd.tensor_copy(cur[:, t % 2, hl], w_hl[:, hl, :, cols]).then_inc(cur_made, 1)

            def add_mask(j, k, c):
                t, h = k * QT + c // NCH, c % NCH
                pool.wait_ge(sim_emptied, sim_unit(j, (k, c))[1] + 1)
                if isinstance(j, int) and j == 0 and k == 0:
                    pool.wait_ge(diagonal_cleared, NT)
                dst = prob[:, (k % 2) * QT + c // NCH, h * CH:(h + 1) * CH]
                src = mask[:, rows(j, t), h * CH:(h + 1) * CH].rearrange("p a m -> p (a m)")
                nc.gpsimd.tensor_tensor(dst, dst, src, ALU.add).then_inc(sim_masked, 1)

            def step1(j, k):
                if isinstance(j, int) and k + 1 >= NB:
                    return
                add_mask(j, k + 1, 0)
                add_mask(j, k + 1, 1)
                if not (isinstance(j, int) and k + 2 >= NB):
                    stage(j, (k + 2) * QT)
                add_mask(j, k + 1, 2)
                add_mask(j, k + 1, 3)
                if not (isinstance(j, int) and k + 2 >= NB):
                    stage(j, (k + 2) * QT + 1)

            stage(0, 0)
            stage(0, 1)
            for c in range(SU):
                add_mask(0, 0, c)
                if c % 2:
                    stage(0, 2 + c // 2)
            step1(0, 0)
            with pool.Fori(0, 2) as j:
                for k in (1, 2):
                    step1(j, k)
            for k in range(5, NB):
                step1(0, k)

        @block.tensor
        def _(pe):
            def take_unit(n):
                if isinstance(n, int) and n < 2:
                    return
                pe.wait_ge(unit_emptied, n - 1)

            def prep(i, slot, n, heads_before):
                take_unit(n)
                pe.wait_ge(parts_made, heads_before * 8 + (i * 2 + 2))
                for t in range(8):
                    mm = pe.transpose(score_ps[:, slot, t * P:(t + 1) * P],
                                      parts[i % 2][:, t, :, :].bitcast(F32).rearrange("p a b -> p (a b)"), ident[:])
                mm.then_inc(unit_filled, 1)

            def scores(s_static, c, slot, n, prep_units):
                b, t = (s_static // NB) % 2, (s_static % NB) * QT + c // NCH
                take_unit(n)
                if prep_units is not None:
                    pe.wait_ge(unit_emptied, prep_units)
                for i in range(CH // 512):
                    c0 = (c % NCH) * CH + i * 512
                    mm = pe.matmul(score_ps[:, slot, i * 512:(i + 1) * 512], q_hl[b][:, t * P:(t + 1) * P],
                                   k_hl[b][:, c0:c0 + 512], start=True, stop=True)
                mm.then_inc(unit_filled, 1)

            def turn(hp, k, u):
                s = hp * BODY + k
                pk, pu = (k, u - 3) if u >= 3 else (k - 1, (6, 7, 5)[u])
                if not (isinstance(s, int) and s == 0 and u < 3):
                    if pu < act_share(pk):
                        pe.wait_ge(act_copied, acts(hp, pk, pu))
                    else:
                        pe.wait_ge(dve_copied, dves(hp, pk, pu))
                elif u == 2:
                    pe.wait_ge(wt_copied, 1)
                if u == 0:
                    pe.wait_ge(tile_exped, s * QT + QT)
                for j in range(JU):
                    for i in range(QT):
                        mm = pe.transpose(turn_ps[u % 3][:, (j * QT + i) * P:(j * QT + i + 1) * P],
                                          prob[:, (k % 2) * QT + i, (u * JU + j) * P:(u * JU + j + 1) * P], ident[:])
                mm.then_inc(turned, 1)

            def finish(slot, n, pairs):
                take_unit(n)
                pe.wait_ge(o_taken, pairs)
                for i in range(2 * QT):
                    mm = pe.transpose(score_ps[:, slot, i * P:(i + 1) * P], o_part[:, i * P:(i + 1) * P], ident[:])
                mm.then_inc(unit_filled, 1)

            def step(hp, k):
                def live(j):
                    return not isinstance(hp, int) or hp * BODY + k + j < STEPS

                def T(u):
                    turn(hp, k, u)

                def V(g, back=0):
                    if g == 0 and k % 2 == 0:
                        pe.wait_ge(o_taken, hp * (BODY // 2) + k // 2)
                    pv_body(hp, k - back, g)

                def S(dk, c):
                    kk = k + dk
                    if live(dk):
                        need = unit(hp, ("prep", kk - NB + PREP_STEPS[-1]))[1] + 1 if kk % NB == 0 and c == 0 else None
                        scores(kk, c, *unit(hp, ("qk", kk, c)), need)

                T(0)
                T(1)
                T(2)
                V(3, 1)
                T(3)
                S(1, 2)
                if k % 2:
                    V(0)
                T(4)
                S(1, 3)
                if k % 2 == 0:
                    finish(*unit(hp, ("fin", k)), hp * (BODY // 2) + k // 2)
                    V(0)
                T(5)
                V(1)
                if k % NB in PREP_STEPS and live(NB - k % NB):
                    heads = hp * 2 + (k // NB + 1)
                    prep(k % NB - PREP_STEPS[0], *unit(hp, ("prep", k)), heads)
                T(6)
                S(2, 0)
                T(7)
                S(2, 1)
                V(2)

            def pv_body(hp, k, g):
                last = 2 * g + 1
                pe.wait_ge(act_copied, acts(hp, k, last))
                if last >= act_share(k):
                    pe.wait_ge(dve_copied, dves(hp, k, last))
                b = (k // NB) % 2
                for q in range(4):
                    j = 4 * g + q
                    mm = pe.matmul(o_ps[HD * q:HD * q + HD, k % 2, :], raw[b][2][:, j, :],
                                   pt[:, j // JU, (j % JU) * QB:(j % JU + 1) * QB],
                                   start=(g == 0 and k % 2 == 0), stop=(g == PVG - 1), skip_group_check=True)
                mm.then_inc(pv_done, 1)

            pe.wait_ge(const_made, 4)
            for i in range(4):
                prep(i, i % 2, i, 0)
            pe.wait_ge(w_landed, 16)
            for it in range(KT):
                for ot in range(KT):
                    mm = pe.transpose(turn_ps[2][:, it * D + ot * P:it * D + (ot + 1) * P],
                                      w_raw[:, ot, it * P:(it + 1) * P], ident[:])
            mm.then_inc(wt_turned, 1)
            for c in range(SU):
                scores(0, c, c % 2, 4 + c, 4 if c == 0 else None)
            for c in range(2):
                scores(1, c, c % 2, 8 + c, None)
            for u in range(TU):
                turn(0, 0, u)
                if u == 3:
                    scores(1, 2, 0, 10, None)
                    pe.wait_ge(raw_in[0], 48)
                    pv_body(0, 0, 0)
                if u == 4:
                    scores(1, 3, 1, 11, None)
                if u == 5:
                    pv_body(0, 0, 1)
                if u == 6:
                    scores(2, 0, 0, 12, None)
            scores(2, 1, 1, 13, None)
            pv_body(0, 0, 2)
            with pe.Fori(0, LOOPS) as hp:
                for k in range(1, BODY + 1):
                    step(hp, k)
            for k in range(1, BODY):
                step(LOOPS, k)
            k = BODY
            pv_body(LOOPS, BODY - 1, 3)
            finish(*unit(LOOPS, ("fin", BODY)), STEPS // 2)

            def seam_x(c, slot):
                pe.wait_ge(x1_made, (c + 1) * CT)
                for kt in range(KT):
                    for t in range(CT):
                        mm = pe.transpose(score_ps[:, slot, kt * CC + t * P:kt * CC + (t + 1) * P],
                                          attn[:, c * CT + t, kt * P:(kt + 1) * P], ident[:])
                mm.then_inc(x1_turned, 1)

            def seam_w(c):
                pe.wait_ge(x1_copied, c + 1)
                if c:
                    pe.wait_ge(lo_taken, KT * c)
                for ot in range(KT):
                    for kt in range(KT):
                        mm = pe.matmul(turn_ps[ot][:], wt[:, kt, ot * P:(ot + 1) * P],
                                       prob[:, 2 + kt, c * CC:(c + 1) * CC], start=(kt == 0), stop=(kt == KT - 1))
                    mm.then_inc(wh_made, 1)

            def seam_s(c):
                pe.wait_ge(squared, KT * (c + 1))
                if c:
                    pe.wait_ge(norm_made, c)
                for ot in range(KT):
                    mm = pe.matmul(turn_ps[2][:], ones[:], prob[:, ot, c * CC:(c + 1) * CC],
                                   start=(ot == 0), stop=(ot == KT - 1))
                mm.then_inc(summed, 1)

            def seam_n(c):
                pe.wait_ge(norm_made, c + 1)
                if c:
                    pe.wait_ge(norm_taken, c)
                for t in range(CT):
                    mm = pe.transpose(o_ps[:].rearrange("p a b -> p (a b)")[:, t * P:(t + 1) * P],
                                      norm_bc[:, c * CC + t * P:c * CC + (t + 1) * P], ident[:])
                mm.then_inc(norm_turned, 1)

            def seam_hl(c, slot, hl):
                pe.wait_ge(lo_taken if hl else hi_taken, KT * (c + 1))
                for t in range(CT):
                    for ot in range(KT):
                        mm = pe.transpose(score_ps[:, slot, t * D + ot * P:t * D + (ot + 1) * P],
                                          w_hl[:, hl, ot, c * CC + t * P:c * CC + (t + 1) * P].bitcast(F32), ident[:])
                mm.then_inc(lo_turned if hl else hi_turned, 1)

            for op in SEAM:
                kind, c = op[0], int(op[1])
                if kind in "xhl":
                    i = SEAM_RING.index(op)
                    if i >= 2:
                        before = SEAM_RING[i - 2]
                        pe.wait_ge(SEAM_FREED[before[0]], int(before[1]) + 1)
                if kind == "x":
                    seam_x(c, i % 2)
                elif kind == "w":
                    seam_w(c)
                elif kind == "s":
                    seam_s(c)
                elif kind == "n":
                    seam_n(c)
                else:
                    seam_hl(c, i % 2, kind == "l")

            def sims(j, k, c):
                slot, n = sim_unit(j, (k, c))
                if isinstance(n, int) and n < 2:
                    before = SEAM_RING[n - 2]
                    pe.wait_ge(SEAM_FREED[before[0]], int(before[1]) + 1)
                else:
                    pe.wait_ge(sim_emptied, n - 1)
                t = k * QT + c // NCH
                pe.wait_ge(cur_made, j * (2 * PAIR * QT) + 2 * (t + 1))
                for i in range(CH // 512):
                    cols = slice((c % NCH) * CH + i * 512, (c % NCH) * CH + (i + 1) * 512)
                    terms = [(a, b, kt) for a, b in ((0, 0), (0, 1), (1, 0)) for kt in range(KT)]
                    for m, (a, b, kt) in enumerate(terms):
                        mm = pe.matmul(score_ps[:, slot, i * 512:(i + 1) * 512], cur[:, t % 2, a, kt, :],
                                       w_hl[:, b, kt, cols], start=(m == 0), stop=(m == len(terms) - 1))
                mm.then_inc(sim_filled, 1)

            def turn1(j, k, u):
                pk, pu = (k, u - 3) if u >= 3 else (k - 1, (6, 7, 5)[u])
                if pk >= 0:
                    pe.wait_ge(lo_copied1, j * (PAIR * TU) + pk * TU + pu + 1)
                elif u == 2:
                    pe.wait_ge(norm_made, NT // CT)
                if u == 0:
                    pe.wait_ge(tile_exped1, j * (PAIR * QT) + (k + 1) * QT)
                for jj in range(JU):
                    for i in range(QT):
                        mm = pe.transpose(turn_ps[u % 3][:, (jj * QT + i) * P:(jj * QT + i + 1) * P],
                                          prob[:, (k % 2) * QT + i, (u * JU + jj) * P:(u * JU + jj + 1) * P], ident[:])
                mm.then_inc(turned1, 1)

            def pv1(j, k, g):
                if g == 0:
                    if k:
                        pe.wait_ge(acc_taken, j * PAIR + k)
                    else:
                        pe.wait_ge(norm_taken, NT // CT)
                        pe.wait_ge(hi_copied, NT // CT)
                        pe.wait_ge(lo_copied, NT // CT)
                pe.wait_ge(lo_copied1, j * (PAIR * TU) + k * TU + 2 * g + 2)
                for q in range(4):
                    t = 4 * g + q
                    u, half = t // JU, t % JU
                    for ot in range(KT):
                        for a, b in ((0, 0), (1, 0), (0, 1)):
                            mm = pe.matmul(o_ps[:, ot, :], wn_hl[:, a, t, ot * P:(ot + 1) * P],
                                           e_hl[:, b, u % 4, half * QB:(half + 1) * QB],
                                           start=(t == 0 and ot == 0 and a + b == 0), stop=(t == NT - 1 and b == 1),
                                           skip_group_check=True)
                mm.then_inc(pv1_done, 1)

            def finish1(j, k):
                slot, n = sim_unit(j, (k, "fin"))
                pe.wait_ge(sim_emptied, n - 1)
                pe.wait_ge(acc_taken, j * PAIR + k + 1)
                for i in range(QT):
                    for ot in range(KT):
                        mm = pe.transpose(score_ps[:, slot, i * D + ot * P:i * D + (ot + 1) * P],
                                          acc_sb[:, ot, i * P:(i + 1) * P], ident[:])
                mm.then_inc(sim_filled, 1)

            def step1(j, k):
                def S(kk, c):
                    if not (isinstance(j, int) and kk >= NB):
                        sims(j, kk, c)
                turn1(j, k, 0)
                turn1(j, k, 1)
                turn1(j, k, 2)
                if k:
                    pv1(j, k - 1, 3)
                turn1(j, k, 3)
                pv1(j, k, 0)
                S(k + 1, 2)
                if k:
                    finish1(j, k - 1)
                turn1(j, k, 4)
                turn1(j, k, 5)
                pv1(j, k, 1)
                S(k + 1, 3)
                turn1(j, k, 6)
                turn1(j, k, 7)
                S(k + 2, 0)
                pv1(j, k, 2)
                S(k + 2, 1)

            for c in range(SU):
                sims(0, 0, c)
            sims(0, 1, 0)
            sims(0, 1, 1)
            step1(0, 0)
            with pe.Fori(0, 2) as j:
                for k in (1, 2):
                    step1(j, k)
            for k in range(5, NB):
                step1(0, k)
            pv1(0, NB - 1, 3)
            finish1(0, NB - 1)

        @block.scalar
        def _(act):
            def exp_tile(n, kk, i):
                act.wait_ge(unit_emptied, n + 1)
                slot = (kk % 2) * QT + i
                r = (kk % 4) * QT + i
                nc.scalar.activation(prob[:, slot, :], prob[:, slot, :], ACT.Exp, bias=neg_max[:, r, 1:2], scale=-1.0,
                                     accum_out=row_sum[:, r:r + 1]).then_inc(tile_exped, 1)

            def copy(s, u, first=False):
                act.wait_ge(turned, s * TU + u + 1)
                if not first:
                    act.wait_ge(pv_done, (s - 1) * PVG + u // 2 + 1)
                nc.scalar.copy(pt[:, u, :], turn_ps[u % 3][:]).then_inc(act_copied, 1)

            def take_o(pairs):
                act.wait_ge(pv_done, pairs * (2 * PVG) + 2 * PVG)
                nc.scalar.copy(o_part[:], o_ps[:].rearrange("p a b -> p (a b)")).then_inc(o_taken, 1)

            def step(hp, k):
                s = hp * BODY + k
                more = not isinstance(s, int) or s + 1 < STEPS
                copy(s, 0)
                copy(s, 1)
                if k % 2 == 0:
                    take_o(hp * (BODY // 2) + (k // 2 - 1))
                copy(s, 2)
                copy(s, 3)
                if more:
                    exp_tile(mask_unit(hp, k + 1, 1)[1], k + 1, 0)
                for u in range(4, act_share(k)):
                    copy(s, u)
                if more:
                    exp_tile(mask_unit(hp, k + 1, 3)[1], k + 1, 1)

            def step0():
                for u in range(4):
                    copy(0, u, True)
                exp_tile(8 + 1, 1, 0)
                for u in range(4, act_share(0)):
                    copy(0, u, True)
                exp_tile(8 + 3, 1, 1)

            act.wait_ge(wt_turned, 1)
            nc.scalar.copy(wt[:].rearrange("p a b -> p (a b)"), turn_ps[2][:]).then_inc(wt_copied, 1)
            exp_tile(4 + 1, 0, 0)
            exp_tile(4 + 3, 0, 1)
            step0()
            with act.Fori(0, LOOPS) as hp:
                for k in range(1, BODY + 1):
                    step(hp, k)
            for k in range(1, BODY):
                step(LOOPS, k)
            take_o(STEPS // 2 - 1)


            def root_var(c):
                act.wait_ge(aggregated, CT * (c + 1))
                if c == 0:
                    act.wait_ge(const_made, 4)
                nc.scalar.activation(rstd[:, c * CT:(c + 1) * CT], mean_var[:, c * CT:(c + 1) * CT, 1], ACT.Sqrt,
                                     bias=eps[:, 1:2]).then_inc(std_made, 1)

            def copy_x1(c):
                slot = SEAM_RING.index(f"x{c}") % 2
                act.wait_ge(x1_turned, c + 1)
                nc.scalar.copy(prob[:, 2:4, c * CC:(c + 1) * CC],
                               score_ps[:, slot, :].rearrange("p (a b) -> p a b", a=KT)).then_inc(x1_copied, 1)

            def take_wh(c):
                for ot in range(KT):
                    act.wait_ge(wh_made, KT * c + ot + 1)
                    nc.scalar.copy(w_hl[:, 0, ot, c * CC:(c + 1) * CC], turn_ps[ot][:]).then_inc(hi_taken, 1)
                for ot in range(KT):
                    nc.scalar.activation(prob[:, ot, c * CC:(c + 1) * CC], turn_ps[ot][:], ACT.Square)\
                        .then_inc(squared, 1)

            def root_norm(c):
                act.wait_ge(summed, c + 1)
                nc.scalar.activation(norm_bc[:, c * CC:(c + 1) * CC], turn_ps[2][:], ACT.Sqrt).then_inc(norm_made, 1)

            def copy_hi(c):
                slot = SEAM_RING.index(f"h{c}") % 2
                act.wait_ge(hi_turned, c + 1)
                nc.scalar.copy(wn_hl[:, 0, c * CT:(c + 1) * CT, :],
                               score_ps[:, slot, :].rearrange("p (a b) -> p a b", a=CT)).then_inc(hi_copied, 1)

            root_var(0)
            root_var(1)
            copy_x1(0)
            root_var(2)
            copy_x1(1)
            root_var(3)
            take_wh(0)
            take_wh(1)
            for c in range(NT // CT):
                root_norm(c)
                copy_hi(c)
                if c + 2 < NT // CT:
                    copy_x1(c + 2)
                    take_wh(c + 2)

            def inv_norms(j, k, i):
                t = k * QT + i
                slot = (k % 2) * QT + i
                if k >= 2 or not isinstance(j, int):
                    act.wait_ge(turned1, j * (PAIR * TU) + (k - 1) * TU)
                elif k == 0 and i == 0:
                    act.wait_ge(norm_taken, NT // CT)
                    act.wait_ge(summed, NT // CT)
                nc.scalar.activation(prob[:, slot, :], norm_bc[:], ACT.Ln, bias=eps[:, 0:1],
                                     scale=norm_col[:, rows(j, t)]).then_inc(log_made, 1)
                act.wait_ge(log_made, j * (PAIR * QT) + t + 1)
                nc.scalar.activation(prob[:, slot, :], prob[:, slot, :], ACT.Exp, scale=-1.0).then_inc(inv_norms_made, 1)

            def exp1(j, k, i):
                t = k * QT + i
                slot = (k % 2) * QT + i
                act.wait_ge(sim_masked, j * (PAIR * SU) + (t + 1) * NCH)
                nc.scalar.activation(prob[:, slot, :], prob[:, slot, :], ACT.Exp,
                                     accum_out=row_sum[:, slot:slot + 1]).then_inc(tile_exped1, 1)

            def copy_e(j, k, u):
                act.wait_ge(turned1, j * (PAIR * TU) + k * TU + u + 1)
                pg = k * PVG + (u - 4) // 2 + 1
                if pg > 0:
                    act.wait_ge(pv1_done, j * (PAIR * PVG) + pg)
                nc.scalar.copy(e_hl[:, 0, u % 4, :], turn_ps[u % 3][:]).then_inc(hi_copied1, 1)

            def root1(j, k):
                act.wait_ge(var_made, j * (PAIR * QT) + (k + 1) * QT)
                nc.scalar.activation(rstd[:, 0:QT], mean_var[:, 0:QT, 1], ACT.Ln, bias=eps[:, 1:2]).then_inc(rstd1_log, 1)
                act.wait_ge(rstd1_log, j * PAIR + k + 1)
                nc.scalar.activation(rstd[:, 0:QT], rstd[:, 0:QT], ACT.Exp, scale=-0.5).then_inc(rstd1_made, 1)

            def step1(j, k):
                more = not (isinstance(j, int) and k + 1 >= NB)
                copy_e(j, k, 0)
                copy_e(j, k, 1)
                copy_e(j, k, 2)
                if more:
                    inv_norms(j, k + 1, 0)
                copy_e(j, k, 3)
                if more:
                    inv_norms(j, k + 1, 1)
                copy_e(j, k, 4)
                copy_e(j, k, 5)
                if k:
                    root1(j, k - 1)
                if more:
                    exp1(j, k + 1, 0)
                copy_e(j, k, 6)
                copy_e(j, k, 7)
                if more:
                    exp1(j, k + 1, 1)

            inv_norms(0, 0, 0)
            inv_norms(0, 0, 1)
            exp1(0, 0, 0)
            exp1(0, 0, 1)
            step1(0, 0)
            with act.Fori(0, 2) as j:
                for k in (1, 2):
                    step1(j, k)
            for k in range(5, NB):
                step1(0, k)
            root1(0, NB - 1)

        @block.vector
        def _(dve):
            def mask_scores(hp, kk, c, slot, n):
                i, h = c // NCH, c % NCH
                t = (kk % NB) * QT + i
                dve.wait_ge(unit_filled, n + 1)
                if c == 0 and not (isinstance(hp, int) and hp * BODY + kk < 2):
                    dve.wait_ge(turned, (hp * BODY + (kk - 1)) * TU)
                r = (kk % 4) * QT + i
                if h:
                    dve.wait_ge(unit_emptied, n)
                stand(dve, dve_passed)
                dve.wait_ge(mask_made, t + 1)
                nc.vector.tensor_tensor_reduce(
                    out=prob[:, (kk % 2) * QT + i, h * CH:(h + 1) * CH], in0=score_ps[:, slot, :],
                    in1=mask[:, t, h * CH:(h + 1) * CH], scale=-1.0,
                    scalar=3.0e38 if h == 0 else neg_max[:, r, 0:1],
                    op0=ALU.add, op1=ALU.min, accum_out=neg_max[:, r, h:h + 1]).then_inc(unit_emptied, 1)

            def make_mask(t):
                dve.wait_ge(adj_landed[t % 2], 16 * (t // 2 + 1))
                nc.vector.tensor_scalar(mask[:, t, :], adj_in[t % 2][:], 0.0, MASKED, ALU.is_le, ALU.mult)\
                    .then_inc(mask_made, 1)

            def prep(i, slot, n, b):
                dve.wait_ge(unit_filled, n + 1)
                dst = (q_hl if i < 2 else k_hl)[b]
                nc.vector.tensor_copy(dst[:, (i % 2) * CH:(i % 2 + 1) * CH], score_ps[:, slot, :])\
                    .then_inc(unit_emptied, 1)

            def copy(s, u, first):
                dve.wait_ge(turned, s * TU + u + 1)
                if not first:
                    dve.wait_ge(pv_done, (s - 1) * PVG + u // 2 + 1)
                nc.vector.tensor_copy(pt[:, u, :], turn_ps[u % 3][:]).then_inc(dve_copied, 1)

            def finish(hp, k, slot, n, pairs):
                r0 = ((k - 2) % 4) * QT
                nc.vector.reciprocal(inv_sum[:], row_sum[:, r0:r0 + 2 * QT]).then_inc(inv_made, 1)
                dve.wait_ge(unit_filled, n + 1)
                dve.wait_ge(inv_made, pairs + 1)
                t0 = ((k - 2) % NB) * QT
                cols = head_cols(hp, k - 2)
                nc.vector.tensor_reduce(o_sum[:], score_ps[:, slot, 0:512].rearrange("p (i g d) -> p i d g", g=4, d=HD),
                                        mybir.AxisListType.X, ALU.add).then_inc(unit_emptied, 1)
                dve.wait_ge(unit_emptied, n + 1)
                nc.vector.tensor_tensor(attn[:, t0:t0 + 2 * QT, cols], o_sum[:],
                                        inv_sum[:].rearrange("p (a b) -> p a b", b=1).broadcast_to([P, 2 * QT, HD]),
                                        ALU.mult).then_inc(attn_made, 1)

            def masks(hp, k, dk, c):
                kk = k + dk
                if isinstance(hp, int) and hp * BODY + kk >= STEPS:
                    return
                mask_scores(hp, kk, c, *mask_unit(hp, kk, c))

            def step(hp, k):
                if k + 1 < NB:
                    if isinstance(hp, int):
                        assert hp
                    else:
                        with dve.If(hp < 1):
                            for i in range(QT):
                                make_mask((k + 1) * QT + i)
                masks(hp, k, 1, 0)
                masks(hp, k, 1, 1)
                masks(hp, k, 1, 2)
                masks(hp, k, 1, 3)
                s = hp * BODY + k
                if k % 2 == 0:
                    slot, n = unit(hp, ("fin", k))
                    finish(hp, k, slot, n, hp * (BODY // 2) + (k // 2 - 1))
                if k % NB in PREP_STEPS and not (isinstance(hp, int) and s + NB - k % NB >= STEPS):
                    slot, n = unit(hp, ("prep", k))
                    prep(k % NB - 2, slot, n, (k // NB + 1) % 2)
                for u in range(act_share(k), TU):
                    copy(s, u, False)

            for i in range(4):
                prep(i, i % 2, i, 0)
            for t in range(2 * QT):
                make_mask(t)
            for c in range(SU):
                mask_scores(0, 0, c, c % 2, 4 + c)
            for c in range(SU):
                mask_scores(0, 1, c, c % 2, 8 + c)
            for u in range(act_share(0), TU):
                copy(0, u, True)
            with dve.Fori(0, LOOPS) as hp:
                for k in range(1, BODY + 1):
                    step(hp, k)
            for k in range(1, BODY):
                step(LOOPS, k)
            finish(LOOPS, BODY, *unit(LOOPS, ("fin", BODY)), STEPS // 2 - 1)


            def row_stats(c):
                dve.wait_ge(x_added, c + 1)
                if c:
                    dve.wait_ge(aggregated, CT * c)
                for t in range(CT):
                    nc.vector.bn_stats(stats[:, t, :], attn[:, c * CT + t, :]).then_inc(stats_made, 1)
                dve.wait_ge(stats_made, CT * (c + 1))
                for t in range(CT):
                    nc.vector.bn_aggr(mean_var[:, c * CT + t, :], stats[:, t, :]).then_inc(aggregated, 1)

            def normalise(c):
                dve.wait_ge(std_made, c + 1)
                nc.vector.reciprocal(rstd[:, c * CT:(c + 1) * CT], rstd[:, c * CT:(c + 1) * CT]).then_inc(rstd_made, 1)
                dve.wait_ge(rstd_made, c + 1)
                for t in range(c * CT, (c + 1) * CT):
                    nc.vector.tensor_scalar(attn[:, t, :], attn[:, t, :], mean_var[:, t, 0:1], rstd[:, t:t + 1],
                                            ALU.subtract, ALU.mult).then_inc(x1_made, 1)

            def take_lo(c):
                for ot in range(KT):
                    dve.wait_ge(squared, KT * c + ot + 1)
                    cols = slice(c * CC, (c + 1) * CC)
                    nc.vector.tensor_tensor(w_hl[:, 1, ot, cols], turn_ps[ot][:], w_hl[:, 0, ot, cols].bitcast(F32),
                                            ALU.subtract).then_inc(lo_taken, 1)

            def copy_lo(c):
                slot = SEAM_RING.index(f"l{c}") % 2
                dve.wait_ge(lo_turned, c + 1)
                nc.vector.tensor_copy(wn_hl[:, 1, c * CT:(c + 1) * CT, :],
                                      score_ps[:, slot, :].rearrange("p (a b) -> p a b", a=CT)).then_inc(lo_copied, 1)

            def take_norm(c):
                dve.wait_ge(norm_turned, c + 1)
                nc.vector.tensor_copy(norm_col[:, c * CT:(c + 1) * CT],
                                      o_ps[:].rearrange("p a (b m) -> p (a b) m", m=P)[:, :, 0]).then_inc(norm_taken, 1)

            row_stats(0)
            row_stats(1)
            normalise(0)
            row_stats(2)
            normalise(1)
            row_stats(3)
            normalise(2)
            normalise(3)
            take_lo(0)
            take_lo(1)
            for c in range(NT // CT):
                copy_lo(c)
                if c:
                    take_norm(c - 1)
                if c + 2 < NT // CT:
                    take_lo(c + 2)
            take_norm(NT // CT - 1)

            def similarity(j, k, c):
                slot, n = sim_unit(j, (k, c))
                dve.wait_ge(inv_norms_made, j * (PAIR * QT) + k * QT + c // NCH + 1)
                dve.wait_ge(sim_filled, n + 1)
                dst = prob[:, (k % 2) * QT + c // NCH, (c % NCH) * CH:(c % NCH + 1) * CH]
                nc.vector.tensor_tensor(dst, score_ps[:, slot, :], dst, ALU.mult).then_inc(sim_emptied, 1)

            def take_e_lo(j, k, u):
                dve.wait_ge(hi_copied1, j * (PAIR * TU) + k * TU + u + 1)
                nc.vector.tensor_tensor(e_hl[:, 1, u % 4, :], turn_ps[u % 3][:], e_hl[:, 0, u % 4, :].bitcast(F32),
                                        ALU.subtract).then_inc(lo_copied1, 1)

            def take_acc(j, k):
                dve.wait_ge(pv1_done, j * (PAIR * PVG) + (k + 1) * PVG)
                nc.vector.tensor_copy(acc_sb[:], o_ps[:]).then_inc(acc_taken, 1)

            def invert_sums(j, k):
                nc.vector.reciprocal(inv_sum[:, 0:QT], row_sum[:, (k % 2) * QT:(k % 2 + 1) * QT]).then_inc(inv1_made, 1)

            def residual(j, k):
                slot, n = sim_unit(j, (k, "fin"))
                dve.wait_ge(sim_filled, n + 1)
                dve.wait_ge(inv1_made, j * PAIR + k + 1)
                for i in range(QT):
                    row = attn[:, rows(j, k * QT + i), :].rearrange("p a d -> p (a d)")
                    ins = nc.vector.scalar_tensor_tensor(out=row, in0=score_ps[:, slot, i * D:(i + 1) * D],
                                                         scalar=inv_sum[:, i:i + 1], in1=row, op0=ALU.mult, op1=ALU.add)
                ins.then_inc(sim_emptied, 1)
                dve.wait_ge(sim_emptied, n + 1)
                stand(dve, dve_passed)
                for i in range(QT):
                    nc.vector.bn_stats(stats[:, i, :], attn[:, rows(j, k * QT + i), :].rearrange("p a d -> p (a d)"))\
                        .then_inc(y_made, 1)
                dve.wait_ge(y_made, j * (PAIR * QT) + (k + 1) * QT)
                stand(dve, dve_passed)
                for i in range(QT):
                    nc.vector.bn_aggr(mean_var[:, i, :], stats[:, i, :]).then_inc(var_made, 1)

            def normalise1(j, k):
                dve.wait_ge(rstd1_made, j * PAIR + k + 1)
                for i in range(QT):
                    row = attn[:, rows(j, k * QT + i), :].rearrange("p a d -> p (a d)")
                    nc.vector.tensor_scalar(row, row, mean_var[:, i, 0:1], rstd[:, i:i + 1],
                                            ALU.subtract, ALU.mult).then_inc(out_made, 1)

            def step1(j, k):
                more = not (isinstance(j, int) and k + 1 >= NB)
                if k:
                    invert_sums(j, k - 1)
                for u in range(3):
                    take_e_lo(j, k, u)
                if k:
                    take_acc(j, k - 1)
                if more:
                    similarity(j, k + 1, 0)
                    similarity(j, k + 1, 1)
                take_e_lo(j, k, 3)
                if more:
                    similarity(j, k + 1, 2)
                if k:
                    residual(j, k - 1)
                take_e_lo(j, k, 4)
                take_e_lo(j, k, 5)
                if more:
                    similarity(j, k + 1, 3)
                take_e_lo(j, k, 6)
                take_e_lo(j, k, 7)
                if k:
                    normalise1(j, k - 1)

            for c in range(SU):
                similarity(0, 0, c)
            step1(0, 0)
            with dve.Fori(0, 2) as j:
                for k in (1, 2):
                    step1(j, k)
            for k in range(5, NB):
                step1(0, k)
            invert_sums(0, NB - 1)
            take_acc(0, NB - 1)
            residual(0, NB - 1)
            normalise1(0, NB - 1)


def kernel(x, adj, L0_gnn_x2, L0_gnn_v, L1_gnn_W):
    import numpy as np
    import concourse.bacc as bacc
    from concourse.bass_utils import run_bass_kernel_spmd

    nc = bacc.Bacc("TRN2", target_bir_lowering=False, num_devices=1)
    arrays, args = {}, []
    for name, a in (("x", x), ("adj", adj), ("x2", L0_gnn_x2), ("v", L0_gnn_v), ("w", L1_gnn_W)):
        a = np.ascontiguousarray(a)
        arrays[f"in_{name}"] = a
        args.append(nc.dram_tensor(f"in_{name}", a.shape, mybir.dt.from_np(a.dtype), kind="ExternalInput").ap())
    args.append(nc.dram_tensor("out_0", x.shape, F32, kind="ExternalOutput").ap())
    build(nc, *args)
    r = run_bass_kernel_spmd(nc, [arrays], core_ids=[0])
    return r.results[0]["out_0"]
```

```python
from contextlib import ExitStack

import concourse.bass as bass
from concourse import mybir

F32 = mybir.dt.float32
F32R = mybir.dt.float32r
BF16 = mybir.dt.bfloat16
I32 = mybir.dt.int32
ALU = mybir.AluOpType
ACT = mybir.ActivationFunctionType

P = 128
LN_EPS = 1e-5
COS_EPS = 1e-8
MASKED = -(2.0 ** 100)
HEADS = 8


def build(nc, x, adj, x2, v, W, out):
    N, D = x.shape
    HD = D // HEADS
    SCALE = HD ** -0.5
    NT = N // P
    KT = D // P
    QT = 2
    QB = QT * P
    NB = N // QB
    STEPS = HEADS * NB
    CH = 1024
    NCH = N // CH
    SU = QT * NCH
    JU = 2
    TU = NT // JU
    PVG = 4
    BODY = 2 * NB
    LOOPS = HEADS // 2 - 1
    assert (HD, NT, KT, NB, SU, TU) == (32, 16, 2, 8, 4, 8)

    xt_dram = x.rearrange("(t p) d -> p t d", p=P)
    kt_dram = x2.rearrange("(t p) d -> p t d", p=P)
    vt_dram = v.rearrange("(t p) d -> p t d", p=P)
    adj_dram = adj.rearrange("(t p) m -> t p m", p=P)
    out_dram = out.rearrange("(t p) d -> p t d", p=P)

    def units_of(k):
        u = [("qk", k + 1, 2), ("qk", k + 1, 3)]
        if k % 2 == 0:
            u.append(("fin", k))
        if k % NB in PREP_STEPS:
            u.append(("prep", k))
        u += [("qk", k + 2, 0), ("qk", k + 2, 1)]
        return u
    PREP_STEPS = (2, 3, 4, 5)
    PRE = [("prep", i) for i in range(4)] + [("qk", 0, c) for c in range(SU)] + [("qk", 1, 0), ("qk", 1, 1)]
    PRE += [("qk", 1, 2), ("qk", 1, 3), ("qk", 2, 0), ("qk", 2, 1)]
    BODY_UNITS = [u for k in range(1, BODY + 1) for u in units_of(k)]
    assert len(PRE) % 2 == 0 and len(BODY_UNITS) % 2 == 0
    def exists(u):
        return LOOPS * BODY + u[1] < STEPS if u[0] == "qk" else u[0] == "fin" or u[1] < NB
    LAST_UNITS = [u for u in BODY_UNITS if exists(u) and u != ("fin", BODY)] + [("fin", BODY)]

    def unit(hp, key):
        units = LAST_UNITS if isinstance(hp, int) and hp == LOOPS else BODY_UNITS
        i = units.index(key)
        return i % 2, hp * len(BODY_UNITS) + (len(PRE) + i)

    def mask_unit(hp, kk, c):
        if kk == 2 and c < 2:
            return c, hp * len(BODY_UNITS) + (len(PRE) - 2 + c)
        return unit(hp, ("qk", kk, c))

    def act_share(k):
        return 6 if k % 2 == 0 else 5

    def acts(hp, k, u):
        before = 11 * (k // 2) + 6 * (k % 2)
        return hp * (11 * BODY // 2) + (before + min(u + 1, act_share(k)))

    def dves(hp, k, u):
        before = 5 * (k // 2) + 2 * (k % 2)
        return hp * (5 * BODY // 2) + (before + max(0, u + 1 - act_share(k)))

    with ExitStack() as ctx:
        def sb(name, shape, dt=F32):
            return ctx.enter_context(nc.sbuf_tensor(name, shape, dt))

        def sem(name):
            return ctx.enter_context(nc.semaphore(name))

        score_ps = ctx.enter_context(nc.psum_tensor("score_ps", [P, 2, CH], F32))
        turn_ps = [ctx.enter_context(nc.psum_tensor(f"turn_ps{i}", [P, 512], F32)) for i in range(3)]
        o_ps = ctx.enter_context(nc.psum_tensor("o_ps", [P, 2, QB], F32))

        mask = sb("mask", [P, NT, N], BF16)
        ident = sb("ident", [P, P])
        ident16 = sb("ident16", [P, P], BF16)
        sum_cols = sb("sum_cols", [P, 2, 2])
        wt = sb("wt", [P, KT, D])
        attn = sb("attn", [P, NT, D])
        prob = sb("prob", [P, 4, N])
        neg_max = sb("neg_max", [P, 8, 2])
        row_sum = sb("row_sum", [P, 8])
        inv_sum = sb("inv_sum", [P, 4])
        stats = sb("stats", [P, 4, 6])
        mean_var = sb("mean_var", [P, NT, 2])
        rstd = sb("rstd", [P, NT])
        norm_col = sb("norm_col", [P, NT])
        eps = sb("eps", [P, 2])

        with ExitStack() as layer0:
            def sb0(name, shape, dt=F32):
                return layer0.enter_context(nc.sbuf_tensor(name, shape, dt))

            q_hl = [sb0(f"q_hl{b}", [P, N], F32R) for b in range(2)]
            k_hl = [sb0(f"k_hl{b}", [P, N], F32R) for b in range(2)]
            pt = sb0("pt", [P, TU, 2 * QB])
            raw = [[sb0(f"raw_{n}{b}", [P, NT, HD]) for n in "qkv"] for b in range(2)]
            scaled = sb0("scaled", [P, NT, HD])
            parts = [sb0(f"parts{i}", [P, NT // 2, 4, HD], F32R) for i in range(2)]
            o_part = sb0("o_part", [P, 2 * QB])
            w_raw = sb0("w_raw", [P, KT, D])
            o_sum = sb0("o_sum", [P, 2 * QT, HD])
            with ExitStack() as masking:
                adj_in = [masking.enter_context(nc.sbuf_tensor(f"adj_in{b}", [P, N], I32)) for b in range(2)]
            x_raw = sb0("x_raw", [P, NT, D])

        w_hl = sb("w_hl", [P, 2, KT, N], F32R)
        wn_hl = sb("wn_hl", [P, 2, NT, D + 2], F32R)
        norm_bc = sb("norm_bc", [P, N])
        e_hl = sb("e_hl", [P, 2, 4, 512], F32R)
        squares = sb("squares", [P, 4, D])

        raw_in = [sem(f"raw_in{b}") for b in range(2)]
        adj_landed = [sem(f"adj_landed{b}") for b in range(2)]
        mask_made = sem("mask_made")
        const_made = sem("const_made")
        const_step = sem("const_step")
        q_scaled = sem("q_scaled")
        hi_made = sem("hi_made")
        parts_made = sem("parts_made")
        unit_filled = sem("unit_filled")
        unit_emptied = sem("unit_emptied")
        tile_exped = sem("tile_exped")
        turned = sem("turned")
        act_copied = sem("act_copied")
        dve_copied = sem("dve_copied")
        pv_done = sem("pv_done")
        o_taken = sem("o_taken")
        attn_made = sem("attn_made")
        inv_made = sem("inv_made")
        dve_passed = sem("dve_passed")
        pool_passed = sem("pool_passed")
        act_passed = sem("act_passed")
        out_done = sem("out_done")
        x_landed, w_landed = sem("x_landed"), sem("w_landed")
        wt_turned, wt_copied = sem("wt_turned"), sem("wt_copied")
        x_added, stats_made, aggregated = sem("x_added"), sem("stats_made"), sem("aggregated")
        log_var, rstd_made, x1_made = sem("log_var"), sem("rstd_made"), sem("x1_made")
        x1_turned, x1_copied = sem("x1_turned"), sem("x1_copied")
        wh_made, hi_taken, lo_taken, wh_joined = sem("wh_made"), sem("hi_taken"), sem("lo_taken"), sem("wh_joined")
        wh_turned, turned_hi, turned_lo, sums_added = sem("wh_turned"), sem("turned_hi"), sem("turned_lo"), sem("sums_added")
        squared, norm_made, norm_turned, norm_spread = sem("squared"), sem("norm_made"), sem("norm_turned"), sem("norm_spread")
        diagonal_cleared = sem("diagonal_cleared")
        sim_filled, sim_scaled, log_made, inv_norms_made = sem("sim_filled"), sem("sim_scaled"), sem("log_made"), sem("inv_norms_made")
        exped, e_hi_made, e_lo_made, pv1_done = sem("exped"), sem("e_hi_made"), sem("e_lo_made"), sem("pv1_done")
        inv1_made, sums_taken, y_made, var_made = sem("inv1_made"), sem("sums_taken"), sem("y_made"), sem("var_made")
        rstd1_log, rstd1_made, out_made = sem("rstd1_log"), sem("rstd1_made"), sem("out_made")

        block = ctx.enter_context(nc.Block())

        def head_cols(hp, k):
            return bass.ds(hp * (2 * HD) + (k // NB) * HD, HD)

        def stand(engine, passed):
            engine.sem_inc(passed, 1)

        CT = 4
        CC = CT * P
        CHUNKS = NT // CT
        SEAM = "x0 fin w0 x1 w1 v0 m0 x2 w2 v1 m1 x3 w3 v2 m2 v3 m3".split()
        SEAM_RING = [u for u in SEAM if u[0] in "xvm"]
        FIN_SLOT, FIN_UNIT = unit(LOOPS, ("fin", BODY))

        def seam_slot(op):
            return (FIN_SLOT + 1 + SEAM_RING.index(op)) % 2

        LN_STEPS = [NB + 2 * c + 3 for c in range(CHUNKS - 1)]
        wh_bank = [turn_ps[0][:], turn_ps[1][:], turn_ps[2][:], o_ps[:].rearrange("p a b -> p (a b)")]

        UNITS1 = NT * CHUNKS
        INV_LEAD, SIM_LEAD, SCALE_LEAD, EXP_LEAD = 4, 3, 2, 1
        SLOTS1 = 8
        ESLOTS = 4

        def exists1(b, t):
            return not isinstance(b, int) or b * NT + t < UNITS1

        def slot1(t):
            return prob[:, 2 + (t % SLOTS1) // 4, (t % 4) * CC:(t % 4 + 1) * CC]

        def sim_bank(t):
            return score_ps[:, (t % 4) // 2, (t % 2) * CC:(t % 2 + 1) * CC]

        def block_rows(b, i, n=1):
            return bass.ds(b * CT + i, n)

        @block.sync
        def _(sp):
            def load_head(cols, b):
                for dst, src in zip(raw[b], (xt_dram, kt_dram, vt_dram)):
                    sp.dma_start(dst[:], src[:, :, cols]).then_inc(raw_in[b], 16)

            load_head(slice(0, HD), 0)
            for t in range(NT):
                if t >= 2:
                    sp.wait_ge(mask_made, t - 1)
                sp.dma_start(adj_in[t % 2][:], adj_dram[t]).then_inc(adj_landed[t % 2], 16)
                if t == 1:
                    load_head(slice(HD, 2 * HD), 1)
                    sp.dma_start(w_raw[:], W.rearrange("(t p) d -> p t d", p=P)).then_inc(w_landed, 16)

            def next_heads(hp, b):
                sp.wait_ge(pv_done, (hp * 2 + (b + 1)) * (NB * PVG))
                load_head(bass.ds(hp * (2 * HD) + (2 + b) * HD, HD), b)

            sp.wait_ge(mask_made, NT)
            sp.dma_start(x_raw[:], xt_dram).then_inc(x_landed, 16)
            with sp.Fori(0, LOOPS) as hp:
                next_heads(hp, 0)
                next_heads(hp, 1)

            def store(b):
                sp.wait_ge(out_made, (b + 1) * CT)
                sp.dma_start(out_dram[:, block_rows(b, 0, CT), :], attn[:, block_rows(b, 0, CT), :]).then_inc(out_done, 16)

            with sp.Fori(0, CHUNKS - 1) as b:
                store(b)
            store(CHUNKS - 1)
            sp.wait_ge(out_done, 16 * CHUNKS)

        @block.gpsimd
        def _(pool):
            nc.gpsimd.memset(ident[:], 0.0).then_inc(const_step, 1)
            pool.wait_ge(const_step, 1)
            nc.gpsimd.affine_select(out=ident[:], in_=ident[:], compare_op=ALU.not_equal, fill=1.0, base=0,
                                    pattern=[[-1, P]], channel_multiplier=1).then_inc(const_made, 1)

            def split(h, i, b, read):
                half = slice((i % 2) * (NT // 2), (i % 2 + 1) * (NT // 2))
                src = scaled[:, half, :] if i < 2 else raw[b][1][:, half, :]
                hi, lo = ((0, 1), (2, 3)) if i < 2 else ((0, 2), (1, 3))
                dst = parts[i % 2]
                pool.wait_ge(q_scaled, h + 1)
                if read is not None:
                    pool.wait_ge(unit_filled, read)
                stand(pool, pool_passed)
                for r in hi:
                    nc.gpsimd.tensor_scalar(dst[:, :, r, :], src, 1.0, 0.0, ALU.mult, ALU.add).then_inc(hi_made, 1)
                pool.wait_ge(hi_made, h * 8 + (i * 2 + 2))
                for r in lo:
                    nc.gpsimd.tensor_tensor(dst[:, :, r, :], src, dst[:, :, hi[0], :].bitcast(F32),
                                            ALU.subtract).then_inc(parts_made, 1)

            def scale_q(h, b, landed, read):
                pool.wait_ge(raw_in[b], landed)
                if read is not None:
                    pool.wait_ge(parts_made, read)
                stand(pool, pool_passed)
                nc.gpsimd.tensor_scalar(scaled[:], raw[b][0][:], SCALE, 0.0, ALU.mult, ALU.add).then_inc(q_scaled, 1)

            pool.wait_ge(const_made, 1)
            nc.gpsimd.tensor_copy(ident16[:], ident[:]).then_inc(const_made, 1)
            nc.gpsimd.memset(sum_cols[:], 0.0).then_inc(const_step, 1)
            pool.wait_ge(const_step, 2)
            nc.gpsimd.memset(sum_cols[:, 0, 0:1], 1.0).then_inc(const_made, 1)
            nc.gpsimd.memset(eps[:, 0:1], COS_EPS).then_inc(const_made, 1)
            nc.gpsimd.memset(eps[:, 1:2], LN_EPS).then_inc(const_made, 1)
            scale_q(0, 0, 48, None)
            for i in range(4):
                split(0, i, 0, None if i < 2 else i - 1)
            scale_q(1, 1, 48, None)
            for i in range(4):
                split(1, i, 1, 3 + i if i < 2 else unit(0, ("prep", i))[1] + 1)

            def body(hp):
                scale_q(hp * 2 + 2, 0, hp * 48 + 96, None)
                for i in range(4):
                    split(hp * 2 + 2, i, 0, unit(hp, ("prep", i + 4 if i < 2 else i + 8))[1] + 1)
                scale_q(hp * 2 + 3, 1, hp * 48 + 96, None)
                for i in range(4):
                    split(hp * 2 + 3, i, 1, (unit(hp, ("prep", i + 12)) if i < 2 else unit(hp + 1, ("prep", i)))[1] + 1)
            with pool.Fori(0, LOOPS) as hp:
                body(hp)

            pool.wait_ge(x_landed, 16)
            for c in range(NT // CT):
                pool.wait_ge(attn_made, (HEADS - 1) * (NB // 2) + c + 1)
                nc.gpsimd.tensor_tensor(attn[:, c * CT:(c + 1) * CT, :], attn[:, c * CT:(c + 1) * CT, :],
                                        x_raw[:, c * CT:(c + 1) * CT, :], ALU.add).then_inc(x_added, 1)
            for t in range(NT):
                block_ = mask[:, t, t * P:(t + 1) * P]
                nc.gpsimd.affine_select(out=block_, in_=block_, compare_op=ALU.not_equal, fill=0.0, base=0,
                                        pattern=[[-1, P]], channel_multiplier=1).then_inc(diagonal_cleared, 1)

            pool.wait_ge(pv_done, STEPS * PVG)
            for hl in range(2):
                nc.gpsimd.tensor_copy(wn_hl[:, hl, :, D:D + 2],
                                      sum_cols[:, hl, :].rearrange("p (a b) -> p a b", a=1).broadcast_to([P, NT, 2]))\
                    .then_inc(sums_added, 1)
            for c in range(CHUNKS):
                for ot in range(KT):
                    pool.wait_ge(lo_taken, KT * c + ot + 1)
                    cols = slice(c * CC, (c + 1) * CC)
                    nc.gpsimd.tensor_tensor(prob[:, ot, cols], w_hl[:, 0, ot, cols].bitcast(F32),
                                            w_hl[:, 1, ot, cols].bitcast(F32), ALU.add).then_inc(wh_joined, 1)

            def e_hi(b, t):
                if not exists1(b, t):
                    return
                pool.wait_ge(exped, b * NT + t + 1)
                if not isinstance(b, int) or b * NT + t >= ESLOTS:
                    pool.wait_ge(pv1_done, b * NT + t - ESLOTS + 1)
                stand(pool, pool_passed)
                nc.gpsimd.tensor_scalar(e_hl[:, 0, t % ESLOTS, :], slot1(t), 1.0, 0.0, ALU.mult, ALU.add)\
                    .then_inc(e_hi_made, 1)

            e_hi(0, 0)
            for t in range(4):
                e_hi(0, t + EXP_LEAD)
            with pool.Fori(0, CHUNKS - 1) as b:
                for t in range(4, NT + 4):
                    e_hi(b, t + EXP_LEAD)
            for t in range(4, NT):
                e_hi(CHUNKS - 1, t + EXP_LEAD)

        @block.tensor
        def _(pe):
            def take_unit(n):
                if isinstance(n, int) and n < 2:
                    return
                pe.wait_ge(unit_emptied, n - 1)

            def prep(i, slot, n, heads_before):
                take_unit(n)
                pe.wait_ge(parts_made, heads_before * 8 + (i * 2 + 2))
                for t in range(8):
                    mm = pe.transpose(score_ps[:, slot, t * P:(t + 1) * P],
                                      parts[i % 2][:, t, :, :].bitcast(F32).rearrange("p a b -> p (a b)"), ident[:])
                mm.then_inc(unit_filled, 1)

            def scores(s_static, c, slot, n, prep_units):
                b, t = (s_static // NB) % 2, (s_static % NB) * QT + c // NCH
                take_unit(n)
                if prep_units is not None:
                    pe.wait_ge(unit_emptied, prep_units)
                for i in range(CH // 512):
                    c0 = (c % NCH) * CH + i * 512
                    mm = pe.matmul(score_ps[:, slot, i * 512:(i + 1) * 512], q_hl[b][:, t * P:(t + 1) * P],
                                   k_hl[b][:, c0:c0 + 512], start=True, stop=True)
                mm.then_inc(unit_filled, 1)

            def turn(hp, k, u):
                s = hp * BODY + k
                pk, pu = (k, u - 3) if u >= 3 else (k - 1, (6, 7, 5)[u])
                if not (isinstance(s, int) and s == 0 and u < 3):
                    if pu < act_share(pk):
                        pe.wait_ge(act_copied, acts(hp, pk, pu))
                    else:
                        pe.wait_ge(dve_copied, dves(hp, pk, pu))
                elif u == 2:
                    pe.wait_ge(wt_copied, 1)
                if u == 0:
                    pe.wait_ge(tile_exped, s * QT + QT)
                for j in range(JU):
                    for i in range(QT):
                        mm = pe.transpose(turn_ps[u % 3][:, (j * QT + i) * P:(j * QT + i + 1) * P],
                                          prob[:, (k % 2) * QT + i, (u * JU + j) * P:(u * JU + j + 1) * P], ident[:])
                mm.then_inc(turned, 1)

            def finish(slot, n, pairs):
                take_unit(n)
                pe.wait_ge(o_taken, pairs)
                for i in range(2 * QT):
                    mm = pe.transpose(score_ps[:, slot, i * P:(i + 1) * P], o_part[:, i * P:(i + 1) * P], ident[:])
                mm.then_inc(unit_filled, 1)

            def step(hp, k):
                def live(j):
                    return not isinstance(hp, int) or hp * BODY + k + j < STEPS

                def T(u):
                    turn(hp, k, u)

                def V(g, back=0):
                    if g == 0 and k % 2 == 0:
                        pe.wait_ge(o_taken, hp * (BODY // 2) + k // 2)
                    pv_body(hp, k - back, g)

                def S(dk, c):
                    kk = k + dk
                    if live(dk):
                        need = unit(hp, ("prep", kk - NB + PREP_STEPS[-1]))[1] + 1 if kk % NB == 0 and c == 0 else None
                        scores(kk, c, *unit(hp, ("qk", kk, c)), need)

                T(0)
                T(1)
                T(2)
                V(3, 1)
                T(3)
                S(1, 2)
                if k % 2:
                    V(0)
                T(4)
                S(1, 3)
                if k % 2 == 0:
                    finish(*unit(hp, ("fin", k)), hp * (BODY // 2) + k // 2)
                    V(0)
                T(5)
                V(1)
                if k % NB in PREP_STEPS and live(NB - k % NB):
                    heads = hp * 2 + (k // NB + 1)
                    prep(k % NB - PREP_STEPS[0], *unit(hp, ("prep", k)), heads)
                T(6)
                S(2, 0)
                T(7)
                S(2, 1)
                V(2)

            def pv_body(hp, k, g):
                last = 2 * g + 1
                pe.wait_ge(act_copied, acts(hp, k, last))
                if last >= act_share(k):
                    pe.wait_ge(dve_copied, dves(hp, k, last))
                b = (k // NB) % 2
                for q in range(4):
                    j = 4 * g + q
                    mm = pe.matmul(o_ps[HD * q:HD * q + HD, k % 2, :], raw[b][2][:, j, :],
                                   pt[:, j // JU, (j % JU) * QB:(j % JU + 1) * QB],
                                   start=(g == 0 and k % 2 == 0), stop=(g == PVG - 1), skip_group_check=True)
                mm.then_inc(pv_done, 1)

            pe.wait_ge(const_made, 5)
            for i in range(4):
                prep(i, i % 2, i, 0)
            pe.wait_ge(w_landed, 16)
            for it in range(KT):
                for ot in range(KT):
                    mm = pe.transpose(turn_ps[2][:, it * D + ot * P:it * D + (ot + 1) * P],
                                      w_raw[:, ot, it * P:(it + 1) * P], ident[:])
            mm.then_inc(wt_turned, 1)
            for c in range(SU):
                scores(0, c, c % 2, 4 + c, 4 if c == 0 else None)
            for c in range(2):
                scores(1, c, c % 2, 8 + c, None)
            for u in range(TU):
                turn(0, 0, u)
                if u == 3:
                    scores(1, 2, 0, 10, None)
                    pe.wait_ge(raw_in[0], 48)
                    pv_body(0, 0, 0)
                if u == 4:
                    scores(1, 3, 1, 11, None)
                if u == 5:
                    pv_body(0, 0, 1)
                if u == 6:
                    scores(2, 0, 0, 12, None)
            scores(2, 1, 1, 13, None)
            pv_body(0, 0, 2)
            with pe.Fori(0, LOOPS) as hp:
                for k in range(1, BODY + 1):
                    step(hp, k)
            for k in range(1, BODY):
                step(LOOPS, k)

            def seam_x(c, slot):
                pe.wait_ge(x1_made, (c + 1) * CT)
                for kt in range(KT):
                    for t in range(CT):
                        mm = pe.transpose(score_ps[:, slot, kt * CC + t * P:kt * CC + (t + 1) * P],
                                          attn[:, c * CT + t, kt * P:(kt + 1) * P], ident[:])
                mm.then_inc(x1_turned, 1)

            def seam_w(c):
                pe.wait_ge(x1_copied, c + 1)
                for ot in range(KT):
                    i = KT * c + ot
                    if i >= len(wh_bank):
                        pe.wait_ge(lo_taken, i - len(wh_bank) + 1)
                    elif i == 0:
                        pe.wait_ge(act_copied, acts(LOOPS, BODY - 1, TU - 1))
                        pe.wait_ge(dve_copied, dves(LOOPS, BODY - 1, TU - 1))
                    elif i == len(wh_bank) - 1:
                        pe.wait_ge(o_taken, STEPS // 2)
                    for kt in range(KT):
                        mm = pe.matmul(wh_bank[i % len(wh_bank)], wt[:, kt, ot * P:(ot + 1) * P],
                                       prob[:, 2 + kt, c * CC:(c + 1) * CC], start=(kt == 0), stop=(kt == KT - 1))
                    mm.then_inc(wh_made, 1)

            def seam_v(c, slot):
                pe.wait_ge(wh_joined, KT * (c + 1))
                for t in range(CT):
                    for ot in range(KT):
                        mm = pe.transpose(score_ps[:, slot, t * D + ot * P:t * D + (ot + 1) * P],
                                          prob[:, ot, c * CC + t * P:c * CC + (t + 1) * P], ident[:])
                mm.then_inc(wh_turned, 1)

            def seam_m(c, slot):
                pe.wait_ge(norm_made, c + 1)
                for t in range(CT):
                    mm = pe.transpose(score_ps[:, slot, t * P:(t + 1) * P],
                                      norm_col[:, c * CT + t:c * CT + t + 1].broadcast_to([P, P]), ident[:])
                mm.then_inc(norm_turned, 1)

            def seam_bank_free(op):
                i = SEAM_RING.index(op)
                if i < 2:
                    pe.wait_ge(unit_emptied, FIN_UNIT + i)
                    return
                kind, c = SEAM_RING[i - 2][0], int(SEAM_RING[i - 2][1])
                if kind == "x":
                    pe.wait_ge(x1_copied, c + 1)
                elif kind == "v":
                    pe.wait_ge(squared, CT * (c + 1))
                    pe.wait_ge(turned_lo, c + 1)
                else:
                    pe.wait_ge(norm_spread, c + 1)

            for op in SEAM:
                if op == "fin":
                    pv_body(LOOPS, BODY - 1, 3)
                    finish(FIN_SLOT, FIN_UNIT, STEPS // 2)
                    continue
                kind, c = op[0], int(op[1])
                if kind == "w":
                    seam_w(c)
                else:
                    seam_bank_free(op)
                    {"x": seam_x, "v": seam_v, "m": seam_m}[kind](c, seam_slot(op))

            def sims(b, t):
                if not exists1(b, t):
                    return
                n = b * NT + t
                if not isinstance(b, int) or n >= 4:
                    pe.wait_ge(sim_scaled, n - 3)
                elif n == 0:
                    pe.wait_ge(norm_spread, CHUNKS)
                    pe.wait_ge(squared, NT)
                    pe.wait_ge(turned_lo, CHUNKS)
                    pe.wait_ge(diagonal_cleared, NT)
                keys, blk = slice((t % NT) * P, (t % NT + 1) * P), b + t // NT
                terms = [(0, 0, 0), (0, 0, 1), (0, 1, 0), (0, 1, 1), (1, 0, 0), (1, 1, 0)]
                for m, (a, kt, q) in enumerate(terms):
                    pe.matmul(sim_bank(t), w_hl[:, a, kt, keys], w_hl[:, q, kt, bass.ds(blk * CC, CC)],
                              start=(m == 0), stop=False, skip_group_check=True)
                for i in range(CT):
                    mm = pe.matmul(sim_bank(t)[:, i * P:(i + 1) * P],
                                   mask[:, block_rows(blk, i), keys].rearrange("p a m -> p (a m)"), ident16[:],
                                   start=False, stop=True, skip_group_check=True)
                mm.then_inc(sim_filled, 1)

            def pv1(b, t):
                n, tk, blk = b * NT + t, t % NT, b + t // NT
                pe.wait_ge(e_hi_made, n + 1)
                pe.wait_ge(e_lo_made, n + 1)
                if isinstance(b, int) and n == 0:
                    pe.wait_ge(turned_hi, CHUNKS)
                    pe.wait_ge(sums_added, 2)
                for i in range(CT):
                    if tk == 0 and not (isinstance(b, int) and blk == 0):
                        pe.wait_ge(sums_taken, (blk - 1) * CT + (i + 1))
                    for m, (a, w) in enumerate(((0, 0), (0, 1), (1, 0))):
                        mm = pe.matmul(wh_bank[i][:, 0:D + 2], e_hl[:, a, t % ESLOTS, i * P:(i + 1) * P], wn_hl[:, w, tk, :],
                                       start=(tk == 0 and m == 0), stop=(tk == NT - 1 and m == 2), skip_group_check=True)
                mm.then_inc(pv1_done, 1)

            def step1(b, t):
                sims(b, t + SIM_LEAD)
                pv1(b, t)

            for t in range(SIM_LEAD):
                sims(0, t)
            for t in range(4):
                step1(0, t)
            with pe.Fori(0, CHUNKS - 1) as b:
                for t in range(4, NT + 4):
                    step1(b, t)
            for t in range(4, NT):
                step1(CHUNKS - 1, t)

        @block.scalar
        def _(act):
            def exp_tile(n, kk, i):
                act.wait_ge(unit_emptied, n + 1)
                slot = (kk % 2) * QT + i
                r = (kk % 4) * QT + i
                nc.scalar.activation(prob[:, slot, :], prob[:, slot, :], ACT.Exp, bias=neg_max[:, r, 1:2], scale=-1.0,
                                     accum_out=row_sum[:, r:r + 1]).then_inc(tile_exped, 1)

            def copy(s, u, first=False):
                act.wait_ge(turned, s * TU + u + 1)
                if not first:
                    act.wait_ge(pv_done, (s - 1) * PVG + u // 2 + 1)
                nc.scalar.copy(pt[:, u, :], turn_ps[u % 3][:]).then_inc(act_copied, 1)

            def take_o(pairs):
                act.wait_ge(pv_done, pairs * (2 * PVG) + 2 * PVG)
                nc.scalar.copy(o_part[:], o_ps[:].rearrange("p a b -> p (a b)")).then_inc(o_taken, 1)

            def step(hp, k):
                s = hp * BODY + k
                more = not isinstance(s, int) or s + 1 < STEPS
                copy(s, 0)
                copy(s, 1)
                if k % 2 == 0:
                    take_o(hp * (BODY // 2) + (k // 2 - 1))
                copy(s, 2)
                copy(s, 3)
                if more:
                    exp_tile(mask_unit(hp, k + 1, 1)[1], k + 1, 0)
                for u in range(4, act_share(k)):
                    copy(s, u)
                if more:
                    exp_tile(mask_unit(hp, k + 1, 3)[1], k + 1, 1)

            def step0():
                for u in range(4):
                    copy(0, u, True)
                exp_tile(8 + 1, 1, 0)
                for u in range(4, act_share(0)):
                    copy(0, u, True)
                exp_tile(8 + 3, 1, 1)

            nc.scalar.preload_act_table_set("natural_log_exp_and_others")
            act.wait_ge(wt_turned, 1)
            nc.scalar.copy(wt[:].rearrange("p a b -> p (a b)"), turn_ps[2][:]).then_inc(wt_copied, 1)
            exp_tile(4 + 1, 0, 0)
            exp_tile(4 + 3, 0, 1)
            step0()
            with act.Fori(0, LOOPS) as hp:
                for k in range(1, BODY + 1):
                    step(hp, k)

            def root_var(c):
                act.wait_ge(aggregated, CT * (c + 1))
                if c == 0:
                    act.wait_ge(const_made, 5)
                nc.scalar.activation(rstd[:, c * CT:(c + 1) * CT], mean_var[:, c * CT:(c + 1) * CT, 1], ACT.Ln,
                                     bias=eps[:, 1:2]).then_inc(log_var, 1)
                act.wait_ge(log_var, c + 1)
                nc.scalar.activation(rstd[:, c * CT:(c + 1) * CT], rstd[:, c * CT:(c + 1) * CT], ACT.Exp,
                                     scale=-0.5).then_inc(rstd_made, 1)

            for k in range(1, BODY):
                step(LOOPS, k)
                if k in LN_STEPS:
                    root_var(LN_STEPS.index(k))

            def copy_x1(c):
                act.wait_ge(x1_turned, c + 1)
                nc.scalar.copy(prob[:, 2:4, c * CC:(c + 1) * CC],
                               score_ps[:, seam_slot(f"x{c}"), :].rearrange("p (a b) -> p a b", a=KT)).then_inc(x1_copied, 1)

            def take_hi(c):
                for ot in range(KT):
                    act.wait_ge(wh_made, KT * c + ot + 1)
                    nc.scalar.copy(w_hl[:, 0, ot, c * CC:(c + 1) * CC], wh_bank[(KT * c + ot) % len(wh_bank)]).then_inc(hi_taken, 1)

            def copy_hi(c):
                act.wait_ge(wh_turned, c + 1)
                nc.scalar.copy(wn_hl[:, 0, c * CT:(c + 1) * CT, 0:D],
                               score_ps[:, seam_slot(f"v{c}"), :].rearrange("p (a b) -> p a b", a=CT)).then_inc(turned_hi, 1)

            def norms(c):
                act.wait_ge(turned_lo, c + 1)
                for t in range(CT):
                    r = c * CT + t
                    nc.scalar.activation(squares[:, t, :], score_ps[:, seam_slot(f"v{c}"), t * D:(t + 1) * D], ACT.Square,
                                         accum_out=norm_col[:, r:r + 1]).then_inc(squared, 1)
                act.wait_ge(squared, CT * (c + 1))
                nc.scalar.activation(norm_col[:, c * CT:(c + 1) * CT], norm_col[:, c * CT:(c + 1) * CT], ACT.Sqrt)\
                    .then_inc(norm_made, 1)

            copy_x1(0)
            take_o(STEPS // 2 - 1)
            take_hi(0)
            copy_x1(1)
            root_var(CHUNKS - 1)
            for c in range(CHUNKS):
                if c + 1 < CHUNKS:
                    take_hi(c + 1)
                copy_hi(c)
                norms(c)
                if c + 2 < CHUNKS:
                    copy_x1(c + 2)

            def log_norms(b, t):
                if not exists1(b, t):
                    return
                n, tk = b * NT + t, t % NT
                if not isinstance(b, int) or n >= SLOTS1:
                    act.wait_ge(e_lo_made, n - SLOTS1 + 1)
                    stand(act, act_passed)
                elif n == 0:
                    act.wait_ge(norm_spread, CHUNKS)
                    act.wait_ge(wh_made, KT * CHUNKS)
                nc.scalar.activation(slot1(t), norm_bc[:, bass.ds((b + t // NT) * CC, CC)], ACT.Ln, bias=eps[:, 0:1],
                                     scale=norm_col[:, tk:tk + 1]).then_inc(log_made, 1)

            def inv_norms(b, t):
                if exists1(b, t):
                    act.wait_ge(log_made, b * NT + t + 1)
                    nc.scalar.activation(slot1(t), slot1(t), ACT.Exp, scale=-1.0).then_inc(inv_norms_made, 1)

            def exp1(b, t):
                if exists1(b, t):
                    act.wait_ge(sim_scaled, b * NT + t + 1)
                    nc.scalar.activation(slot1(t), slot1(t), ACT.Exp).then_inc(exped, 1)

            def root1(b):
                act.wait_ge(var_made, (b + 1) * CT)
                nc.scalar.activation(rstd[:, 0:CT], mean_var[:, 0:CT, 1], ACT.Ln, bias=eps[:, 1:2]).then_inc(rstd1_log, 1)
                act.wait_ge(rstd1_log, b + 1)
                nc.scalar.activation(rstd[:, 0:CT], rstd[:, 0:CT], ACT.Exp, scale=-0.5).then_inc(rstd1_made, 1)

            def step1(b, t):
                log_norms(b, t + INV_LEAD)
                exp1(b, t + EXP_LEAD)
                inv_norms(b, t + INV_LEAD)
                if t == NT + 2:
                    root1(b)

            nc.scalar.preload_act_table_set("natural_log_exp_and_others")
            for t in range(INV_LEAD):
                log_norms(0, t)
                inv_norms(0, t)
            exp1(0, 0)
            for t in range(4):
                step1(0, t)
            with act.Fori(0, CHUNKS - 1) as b:
                for t in range(4, NT + 4):
                    step1(b, t)
            for t in range(4, NT):
                step1(CHUNKS - 1, t)
            root1(CHUNKS - 1)

        @block.vector
        def _(dve):
            def mask_scores(hp, kk, c, slot, n):
                i, h = c // NCH, c % NCH
                t = (kk % NB) * QT + i
                dve.wait_ge(unit_filled, n + 1)
                if c == 0 and not (isinstance(hp, int) and hp * BODY + kk < 2):
                    dve.wait_ge(turned, (hp * BODY + (kk - 1)) * TU)
                r = (kk % 4) * QT + i
                if h:
                    dve.wait_ge(unit_emptied, n)
                stand(dve, dve_passed)
                dve.wait_ge(mask_made, t + 1)
                nc.vector.tensor_tensor_reduce(
                    out=prob[:, (kk % 2) * QT + i, h * CH:(h + 1) * CH], in0=score_ps[:, slot, :],
                    in1=mask[:, t, h * CH:(h + 1) * CH], scale=-1.0,
                    scalar=3.0e38 if h == 0 else neg_max[:, r, 0:1],
                    op0=ALU.add, op1=ALU.min, accum_out=neg_max[:, r, h:h + 1]).then_inc(unit_emptied, 1)

            def make_mask(t):
                dve.wait_ge(adj_landed[t % 2], 16 * (t // 2 + 1))
                nc.vector.tensor_scalar(mask[:, t, :], adj_in[t % 2][:], 0.0, MASKED, ALU.is_le, ALU.mult)\
                    .then_inc(mask_made, 1)

            def prep(i, slot, n, b):
                dve.wait_ge(unit_filled, n + 1)
                dst = (q_hl if i < 2 else k_hl)[b]
                nc.vector.tensor_copy(dst[:, (i % 2) * CH:(i % 2 + 1) * CH], score_ps[:, slot, :])\
                    .then_inc(unit_emptied, 1)

            def copy(s, u, first):
                dve.wait_ge(turned, s * TU + u + 1)
                if not first:
                    dve.wait_ge(pv_done, (s - 1) * PVG + u // 2 + 1)
                nc.vector.tensor_copy(pt[:, u, :], turn_ps[u % 3][:]).then_inc(dve_copied, 1)

            def finish(hp, k, slot, n, pairs):
                r0 = ((k - 2) % 4) * QT
                nc.vector.reciprocal(inv_sum[:], row_sum[:, r0:r0 + 2 * QT]).then_inc(inv_made, 1)
                dve.wait_ge(unit_filled, n + 1)
                dve.wait_ge(inv_made, pairs + 1)
                t0 = ((k - 2) % NB) * QT
                cols = head_cols(hp, k - 2)
                nc.vector.tensor_reduce(o_sum[:], score_ps[:, slot, 0:512].rearrange("p (i g d) -> p i d g", g=4, d=HD),
                                        mybir.AxisListType.X, ALU.add).then_inc(unit_emptied, 1)
                dve.wait_ge(unit_emptied, n + 1)
                nc.vector.tensor_tensor(attn[:, t0:t0 + 2 * QT, cols], o_sum[:],
                                        inv_sum[:].rearrange("p (a b) -> p a b", b=1).broadcast_to([P, 2 * QT, HD]),
                                        ALU.mult).then_inc(attn_made, 1)

            def masks(hp, k, dk, c):
                kk = k + dk
                if isinstance(hp, int) and hp * BODY + kk >= STEPS:
                    return
                mask_scores(hp, kk, c, *mask_unit(hp, kk, c))

            def step(hp, k):
                if k + 1 < NB:
                    if isinstance(hp, int):
                        assert hp
                    else:
                        with dve.If(hp < 1):
                            for i in range(QT):
                                make_mask((k + 1) * QT + i)
                masks(hp, k, 1, 0)
                masks(hp, k, 1, 1)
                masks(hp, k, 1, 2)
                masks(hp, k, 1, 3)
                s = hp * BODY + k
                if k % 2 == 0:
                    slot, n = unit(hp, ("fin", k))
                    finish(hp, k, slot, n, hp * (BODY // 2) + (k // 2 - 1))
                if k % NB in PREP_STEPS and not (isinstance(hp, int) and s + NB - k % NB >= STEPS):
                    slot, n = unit(hp, ("prep", k))
                    prep(k % NB - 2, slot, n, (k // NB + 1) % 2)
                for u in range(act_share(k), TU):
                    copy(s, u, False)

            for i in range(4):
                prep(i, i % 2, i, 0)
            for t in range(2 * QT):
                make_mask(t)
            for c in range(SU):
                mask_scores(0, 0, c, c % 2, 4 + c)
            for c in range(SU):
                mask_scores(0, 1, c, c % 2, 8 + c)
            for u in range(act_share(0), TU):
                copy(0, u, True)
            with dve.Fori(0, LOOPS) as hp:
                for k in range(1, BODY + 1):
                    step(hp, k)

            def row_stats(c):
                dve.wait_ge(x_added, c + 1)
                if c:
                    dve.wait_ge(aggregated, CT * c)
                for t in range(CT):
                    nc.vector.bn_stats(stats[:, t, :], attn[:, c * CT + t, :]).then_inc(stats_made, 1)
                dve.wait_ge(stats_made, CT * (c + 1))
                for t in range(CT):
                    nc.vector.bn_aggr(mean_var[:, c * CT + t, :], stats[:, t, :]).then_inc(aggregated, 1)

            def normalise(c):
                dve.wait_ge(rstd_made, c + 1)
                for t in range(c * CT, (c + 1) * CT):
                    nc.vector.tensor_scalar(attn[:, t, :], attn[:, t, :], mean_var[:, t, 0:1], rstd[:, t:t + 1],
                                            ALU.subtract, ALU.mult).then_inc(x1_made, 1)

            for k in range(1, BODY):
                step(LOOPS, k)
                if k in LN_STEPS:
                    row_stats(LN_STEPS.index(k))
                if k - 1 in LN_STEPS and k - 1 != LN_STEPS[-1]:
                    normalise(LN_STEPS.index(k - 1))
            normalise(len(LN_STEPS) - 1)
            finish(LOOPS, BODY, FIN_SLOT, FIN_UNIT, STEPS // 2 - 1)

            def take_lo(c):
                for ot in range(KT):
                    dve.wait_ge(hi_taken, KT * c + ot + 1)
                    cols = slice(c * CC, (c + 1) * CC)
                    nc.vector.tensor_tensor(w_hl[:, 1, ot, cols], wh_bank[(KT * c + ot) % len(wh_bank)],
                                            w_hl[:, 0, ot, cols].bitcast(F32), ALU.subtract).then_inc(lo_taken, 1)

            def turn_lo(c):
                dve.wait_ge(turned_hi, c + 1)
                rows = slice(c * CT, (c + 1) * CT)
                nc.vector.tensor_tensor(wn_hl[:, 1, rows, 0:D], score_ps[:, seam_slot(f"v{c}"), :].rearrange("p (a b) -> p a b", a=CT),
                                        wn_hl[:, 0, rows, 0:D].bitcast(F32), ALU.subtract).then_inc(turned_lo, 1)

            def spread_norm(c):
                dve.wait_ge(norm_turned, c + 1)
                nc.vector.tensor_copy(norm_bc[:, c * CC:(c + 1) * CC], score_ps[:, seam_slot(f"m{c}"), 0:CC]).then_inc(norm_spread, 1)

            take_lo(0)
            row_stats(CHUNKS - 1)
            normalise(CHUNKS - 1)
            for c in range(CHUNKS):
                if c + 1 < CHUNKS:
                    take_lo(c + 1)
                turn_lo(c)
                spread_norm(c)

            def scale(b, t):
                if not exists1(b, t):
                    return
                dve.wait_ge(inv_norms_made, b * NT + t + 1)
                dve.wait_ge(sim_filled, b * NT + t + 1)
                nc.vector.tensor_tensor(slot1(t), sim_bank(t), slot1(t), ALU.mult).then_inc(sim_scaled, 1)

            def e_lo(b, t):
                if not exists1(b, t):
                    return
                dve.wait_ge(e_hi_made, b * NT + t + 1)
                nc.vector.tensor_tensor(e_hl[:, 1, t % ESLOTS, :], slot1(t), e_hl[:, 0, t % ESLOTS, :].bitcast(F32),
                                        ALU.subtract).then_inc(e_lo_made, 1)

            def residual(b):
                dve.wait_ge(pv1_done, (b + 1) * NT)
                for i in range(CT):
                    nc.vector.reciprocal(inv_sum[:, i:i + 1], wh_bank[i][:, D:D + 1]).then_inc(inv1_made, 1)
                for i in range(CT):
                    row = attn[:, block_rows(b, i), :].rearrange("p a d -> p (a d)")
                    dve.wait_ge(inv1_made, b * CT + (i + 1))
                    nc.vector.scalar_tensor_tensor(out=row, in0=wh_bank[i][:, 0:D], scalar=inv_sum[:, i:i + 1], in1=row,
                                                   op0=ALU.mult, op1=ALU.add).then_inc(sums_taken, 1)
                dve.wait_ge(sums_taken, (b + 1) * CT)
                stand(dve, dve_passed)
                for i in range(CT):
                    nc.vector.bn_stats(stats[:, i, :], attn[:, block_rows(b, i), :].rearrange("p a d -> p (a d)"))\
                        .then_inc(y_made, 1)
                dve.wait_ge(y_made, (b + 1) * CT)
                stand(dve, dve_passed)
                for i in range(CT):
                    nc.vector.bn_aggr(mean_var[:, i, :], stats[:, i, :]).then_inc(var_made, 1)

            def normalise1(b):
                dve.wait_ge(rstd1_made, b + 1)
                for i in range(CT):
                    row = attn[:, block_rows(b, i), :].rearrange("p a d -> p (a d)")
                    nc.vector.tensor_scalar(row, row, mean_var[:, i, 0:1], rstd[:, i:i + 1],
                                            ALU.subtract, ALU.mult).then_inc(out_made, 1)

            def step1(b, t):
                scale(b, t + SCALE_LEAD)
                e_lo(b, t + EXP_LEAD)
                if t == NT - 1:
                    residual(b)
                if t == NT + 2:
                    normalise1(b)

            scale(0, 0)
            scale(0, 1)
            e_lo(0, 0)
            for t in range(4):
                step1(0, t)
            with dve.Fori(0, CHUNKS - 1) as b:
                for t in range(4, NT + 4):
                    step1(b, t)
            for t in range(4, NT):
                step1(CHUNKS - 1, t)
            normalise1(CHUNKS - 1)


def kernel(x, adj, L0_gnn_x2, L0_gnn_v, L1_gnn_W):
    import numpy as np
    import concourse.bacc as bacc
    from concourse.bass_utils import run_bass_kernel_spmd

    nc = bacc.Bacc("TRN2", target_bir_lowering=False, num_devices=1)
    arrays, args = {}, []
    for name, a in (("x", x), ("adj", adj), ("x2", L0_gnn_x2), ("v", L0_gnn_v), ("w", L1_gnn_W)):
        a = np.ascontiguousarray(a)
        arrays[f"in_{name}"] = a
        args.append(nc.dram_tensor(f"in_{name}", a.shape, mybir.dt.from_np(a.dtype), kind="ExternalInput").ap())
    args.append(nc.dram_tensor("out_0", x.shape, F32, kind="ExternalOutput").ap())
    build(nc, *args)
    r = run_bass_kernel_spmd(nc, [arrays], core_ids=[0])
    return r.results[0]["out_0"]
```

```python
from contextlib import ExitStack

import concourse.bass as bass
from concourse import mybir

F32 = mybir.dt.float32
F32R = mybir.dt.float32r
BF16 = mybir.dt.bfloat16
I32 = mybir.dt.int32
ALU = mybir.AluOpType
ACT = mybir.ActivationFunctionType

P = 128
LN_EPS = 1e-5
TINY = 2.0 ** -126
COS_EPS = 1e-8
MASKED = -(2.0 ** 100)
HEADS = 8


def build(nc, x, adj, x2, v, W, out):
    N, D = x.shape
    HD = D // HEADS
    SCALE = HD ** -0.5
    NT = N // P
    KT = D // P
    QT = 2
    QB = QT * P
    NB = N // QB
    STEPS = HEADS * NB
    CH = 1024
    NCH = N // CH
    SU = QT * NCH
    JU = 2
    TU = NT // JU
    PVG = 4
    BODY = 2 * NB
    LOOPS = HEADS // 2 - 1
    assert (HD, NT, KT, NB, SU, TU) == (32, 16, 2, 8, 4, 8)

    xt_dram = x.rearrange("(t p) d -> p t d", p=P)
    kt_dram = x2.rearrange("(t p) d -> p t d", p=P)
    vt_dram = v.rearrange("(t p) d -> p t d", p=P)
    adj_dram = adj.rearrange("(t p) m -> t p m", p=P)
    out_dram = out.rearrange("(t p) d -> p t d", p=P)

    def units_of(k):
        u = [("qk", k + 1, 2), ("qk", k + 1, 3)]
        if k % 2 == 0:
            u.append(("fin", k))
        if k % NB in PREP_STEPS:
            u.append(("prep", k))
        u += [("qk", k + 2, 0), ("qk", k + 2, 1)]
        return u
    PREP_STEPS = (2, 3, 4, 5)
    PRE = [("prep", i) for i in range(4)] + [("qk", 0, c) for c in range(SU)] + [("qk", 1, 0), ("qk", 1, 1)]
    PRE += [("qk", 1, 2), ("qk", 1, 3), ("qk", 2, 0), ("qk", 2, 1)]
    BODY_UNITS = [u for k in range(1, BODY + 1) for u in units_of(k)]
    assert len(PRE) % 2 == 0 and len(BODY_UNITS) % 2 == 0
    def exists(u):
        return LOOPS * BODY + u[1] < STEPS if u[0] == "qk" else u[0] == "fin" or u[1] < NB
    LAST_UNITS = [u for u in BODY_UNITS if exists(u) and u != ("fin", BODY)] + [("fin", BODY)]

    def unit(hp, key):
        units = LAST_UNITS if isinstance(hp, int) and hp == LOOPS else BODY_UNITS
        i = units.index(key)
        return i % 2, hp * len(BODY_UNITS) + (len(PRE) + i)

    def mask_unit(hp, kk, c):
        if kk == 2 and c < 2:
            return c, hp * len(BODY_UNITS) + (len(PRE) - 2 + c)
        return unit(hp, ("qk", kk, c))

    PE_ORDER = "T0 T1 V31 T2 T3 S12 V0 T4 S13 T5 V1 F P T6 S20 T7 V2 S21"

    ACT_ORDER = "C0 C1 O0 C2 C3 E0 C4 C5 C6 C7 E1"

    DVE_ORDER = "M0 M1 M2 M3 F0 P0 C4 C5 C6 C7"

    DVE_UNITS = [(6, 7), (5, 6, 7), (6, 7), (6, 7), (6, 7), (6, 7), (6, 7), (5, 6, 7)] * 2

    def by_dve(k, u):
        return u in DVE_UNITS[k % BODY]

    DVE_TURNS = sum(len(units) for units in DVE_UNITS)
    ACT_TURNS = TU * BODY - DVE_TURNS

    def dves(hp, k, u):
        before = sum(by_dve(i, w) for i in range(k) for w in range(TU))
        return hp * DVE_TURNS + (before + sum(by_dve(k, w) for w in range(u + 1)))

    def acts(hp, k, u):
        before = sum(not by_dve(i, w) for i in range(k) for w in range(TU))
        return hp * ACT_TURNS + (before + sum(not by_dve(k, w) for w in range(u + 1)))

    with ExitStack() as ctx:
        def sb(name, shape, dt=F32):
            return ctx.enter_context(nc.sbuf_tensor(name, shape, dt))

        def sem(name):
            return ctx.enter_context(nc.semaphore(name))

        score_ps = ctx.enter_context(nc.psum_tensor("score_ps", [P, 2, CH], F32))
        turn_ps = [ctx.enter_context(nc.psum_tensor(f"turn_ps{i}", [P, 512], F32)) for i in range(3)]
        o_ps = ctx.enter_context(nc.psum_tensor("o_ps", [P, 2, QB], F32))

        mask = sb("mask", [P, NT, N], BF16)
        ident = sb("ident", [P, P])
        ident16 = sb("ident16", [P, P], BF16)
        sum_cols = sb("sum_cols", [P, 2, 2])
        wt = sb("wt", [P, KT, D])
        attn = sb("attn", [P, NT, D])
        prob = sb("prob", [P, 4, N])
        neg_max = sb("neg_max", [P, 8, 2])
        row_sum = sb("row_sum", [P, 8])
        inv_sum = sb("inv_sum", [P, 4])
        stats = sb("stats", [P, 4, 6])
        mean_var = sb("mean_var", [P, NT, 2])
        rstd = sb("rstd", [P, NT])
        norm_col = sb("norm_col", [P, NT])
        eps = sb("eps", [P, 3])

        with ExitStack() as layer0:
            def sb0(name, shape, dt=F32):
                return layer0.enter_context(nc.sbuf_tensor(name, shape, dt))

            q_hl = [sb0(f"q_hl{b}", [P, N], F32R) for b in range(2)]
            k_hl = [sb0(f"k_hl{b}", [P, N], F32R) for b in range(2)]
            pt = sb0("pt", [P, TU, 2 * QB])
            raw = [[sb0(f"raw_{n}{b}", [P, NT, HD]) for n in "qkv"] for b in range(2)]
            scaled = sb0("scaled", [P, NT, HD])
            parts = [sb0(f"parts{i}", [P, NT // 2, 4, HD], F32R) for i in range(2)]
            o_part = sb0("o_part", [P, 2 * QB])
            w_raw = sb0("w_raw", [P, KT, D])
            o_sum = sb0("o_sum", [P, 2 * QT, HD])
            with ExitStack() as masking:
                adj_in = [masking.enter_context(nc.sbuf_tensor(f"adj_in{b}", [P, N], I32)) for b in range(2)]
            x_raw = sb0("x_raw", [P, NT, D])

        w_hl = sb("w_hl", [P, 2, KT, N], F32R)
        wn_hl = sb("wn_hl", [P, 2, NT, D + 2], F32R)
        norm_bc = sb("norm_bc", [P, N])
        e_hl = sb("e_hl", [P, 2, 4, 512], F32R)
        squares = sb("squares", [P, 4, D])

        raw_in = [sem(f"raw_in{b}") for b in range(2)]
        adj_landed = [sem(f"adj_landed{b}") for b in range(2)]
        mask_made = sem("mask_made")
        const_made = sem("const_made")
        const_step = sem("const_step")
        q_scaled = sem("q_scaled")
        hi_made = sem("hi_made")
        parts_made = sem("parts_made")
        unit_filled = sem("unit_filled")
        unit_emptied = sem("unit_emptied")
        tile_exped = sem("tile_exped")
        turned = sem("turned")
        act_copied = sem("act_copied")
        dve_copied = sem("dve_copied")
        pv_done = sem("pv_done")
        o_taken = sem("o_taken")
        attn_made = sem("attn_made")
        inv_made = sem("inv_made")
        dve_passed = sem("dve_passed")
        pool_passed = sem("pool_passed")
        act_passed = sem("act_passed")
        out_done = sem("out_done")
        x_landed, w_landed = sem("x_landed"), sem("w_landed")
        wt_turned, wt_copied = sem("wt_turned"), sem("wt_copied")
        x_added, stats_made, aggregated = sem("x_added"), sem("stats_made"), sem("aggregated")
        log_var, rstd_made, x1_made = sem("log_var"), sem("rstd_made"), sem("x1_made")
        x1_turned, x1_copied = sem("x1_turned"), sem("x1_copied")
        wh_made, hi_taken, lo_taken, wh_joined = sem("wh_made"), sem("hi_taken"), sem("lo_taken"), sem("wh_joined")
        wh_turned, turned_hi, turned_lo, sums_added = sem("wh_turned"), sem("turned_hi"), sem("turned_lo"), sem("sums_added")
        log_square = sem("log_square")
        squared, norm_made, norm_turned, norm_spread = sem("squared"), sem("norm_made"), sem("norm_turned"), sem("norm_spread")
        diagonal_cleared = sem("diagonal_cleared")
        sim_filled, sim_scaled, log_made, inv_norms_made = sem("sim_filled"), sem("sim_scaled"), sem("log_made"), sem("inv_norms_made")
        exped, e_hi_made, e_lo_made, pv1_done = sem("exped"), sem("e_hi_made"), sem("e_lo_made"), sem("pv1_done")
        inv1_made, sums_taken, y_made, var_made = sem("inv1_made"), sem("sums_taken"), sem("y_made"), sem("var_made")
        rstd1_log, rstd1_made, out_made = sem("rstd1_log"), sem("rstd1_made"), sem("out_made")

        block = ctx.enter_context(nc.Block())

        def head_cols(hp, k):
            return bass.ds(hp * (2 * HD) + (k // NB) * HD, HD)

        def stand(engine, passed):
            engine.sem_inc(passed, 1)

        CT = 4
        CC = CT * P
        CHUNKS = NT // CT
        SEAM = "x0 fin w0 x1 x2 w1 x3 w2 v0 v1 w3 m0 v2 m1".split()
        SEAM_END = "v3 m2 m3".split()
        FIN_SLOT, FIN_UNIT = unit(LOOPS, ("fin", BODY))
        OTHER = 1 - FIN_SLOT
        X_PAIR = [OTHER, FIN_SLOT, OTHER, FIN_SLOT]

        LN_STEPS = [NB + 2 * c + 3 for c in range(CHUNKS - 1)]
        wh_bank = [turn_ps[0][:], turn_ps[1][:], turn_ps[2][:], o_ps[:].rearrange("p a b -> p (a b)")]

        def v_bank(c, h):
            bank = score_ps[:, X_PAIR[c], h * 512:(h + 1) * 512] if c < 2 else wh_bank[(c - 2) * 2 + h]
            return bank.rearrange("p (a b) -> p a b", a=CT // 2)

        def m_bank(c):
            return score_ps[:, OTHER, (c % 2) * 512:(c % 2 + 1) * 512]

        UNITS1 = NT * CHUNKS
        INV_LEAD, SIM_LEAD, SCALE_LEAD, EXP_LEAD = 4, 3, 2, 1
        SLOTS1 = 8
        ESLOTS = 4

        def exists1(b, t):
            return not isinstance(b, int) or b * NT + t < UNITS1

        def slot1(t):
            return prob[:, 2 + (t % SLOTS1) // 4, (t % 4) * CC:(t % 4 + 1) * CC]

        def sim_bank(t):
            return score_ps[:, ((t % 4) // 2 + FIN_SLOT) % 2, (t % 2) * CC:(t % 2 + 1) * CC]

        def block_rows(b, i, n=1):
            return bass.ds(b * CT + i, n)

        @block.sync
        def _(sp):
            def load_head(cols, b):
                for dst, src in zip(raw[b], (xt_dram, kt_dram, vt_dram)):
                    sp.dma_start(dst[:], src[:, :, cols]).then_inc(raw_in[b], 16)

            load_head(slice(0, HD), 0)
            sp.dma_start(w_raw[:], W.rearrange("(t p) d -> p t d", p=P)).then_inc(w_landed, 16)
            for t in range(NT):
                if t >= 2:
                    sp.wait_ge(mask_made, t - 1)
                sp.dma_start(adj_in[t % 2][:], adj_dram[t]).then_inc(adj_landed[t % 2], 16)
                if t == 2 * QT - 1:
                    load_head(slice(HD, 2 * HD), 1)

            def next_heads(hp, b):
                sp.wait_ge(pv_done, (hp * 2 + (b + 1)) * (NB * PVG))
                load_head(bass.ds(hp * (2 * HD) + (2 + b) * HD, HD), b)

            sp.wait_ge(mask_made, NT)
            sp.dma_start(x_raw[:], xt_dram).then_inc(x_landed, 16)
            with sp.Fori(0, LOOPS) as hp:
                next_heads(hp, 0)
                next_heads(hp, 1)

            def store(b):
                sp.wait_ge(out_made, (b + 1) * CT)
                sp.dma_start(out_dram[:, block_rows(b, 0, CT), :], attn[:, block_rows(b, 0, CT), :]).then_inc(out_done, 16)

            with sp.Fori(0, CHUNKS - 1) as b:
                store(b)
            for half in range(2):
                sp.wait_ge(out_made, (CHUNKS - 1) * CT + (half + 1) * (CT // 2))
                rows = slice((CHUNKS - 1) * CT + half * (CT // 2), (CHUNKS - 1) * CT + (half + 1) * (CT // 2))
                sp.dma_start(out_dram[:, rows, :], attn[:, rows, :]).then_inc(out_done, 16)
            sp.wait_ge(out_done, 16 * (CHUNKS + 1))

        @block.gpsimd
        def _(pool):
            nc.gpsimd.memset(ident[:], 0.0).then_inc(const_step, 1)
            pool.wait_ge(const_step, 1)
            nc.gpsimd.affine_select(out=ident[:], in_=ident[:], compare_op=ALU.not_equal, fill=1.0, base=0,
                                    pattern=[[-1, P]], channel_multiplier=1).then_inc(const_made, 1)

            def split(h, i, b, read):
                half = slice((i % 2) * (NT // 2), (i % 2 + 1) * (NT // 2))
                src = scaled[:, half, :] if i < 2 else raw[b][1][:, half, :]
                hi, lo = ((0, 1), (2, 3)) if i < 2 else ((0, 2), (1, 3))
                dst = parts[i % 2]
                pool.wait_ge(q_scaled, h + 1)
                if read is not None:
                    pool.wait_ge(unit_filled, read)
                stand(pool, pool_passed)
                for r in hi:
                    nc.gpsimd.tensor_scalar(dst[:, :, r, :], src, 1.0, 0.0, ALU.mult, ALU.add).then_inc(hi_made, 1)
                pool.wait_ge(hi_made, h * 8 + (i * 2 + 2))
                for r in lo:
                    nc.gpsimd.tensor_tensor(dst[:, :, r, :], src, dst[:, :, hi[0], :].bitcast(F32),
                                            ALU.subtract).then_inc(parts_made, 1)

            def scale_q(h, b, landed, read):
                pool.wait_ge(raw_in[b], landed)
                if read is not None:
                    pool.wait_ge(parts_made, read)
                stand(pool, pool_passed)
                nc.gpsimd.tensor_scalar(scaled[:], raw[b][0][:], SCALE, 0.0, ALU.mult, ALU.add).then_inc(q_scaled, 1)

            pool.wait_ge(const_made, 1)
            nc.gpsimd.tensor_copy(ident16[:], ident[:]).then_inc(const_made, 1)
            nc.gpsimd.memset(sum_cols[:], 0.0).then_inc(const_step, 1)
            pool.wait_ge(const_step, 2)
            nc.gpsimd.memset(sum_cols[:, 0, 0:1], 1.0).then_inc(const_made, 1)
            nc.gpsimd.memset(eps[:, 0:1], COS_EPS).then_inc(const_made, 1)
            nc.gpsimd.memset(eps[:, 1:2], LN_EPS).then_inc(const_made, 1)
            nc.gpsimd.memset(eps[:, 2:3], TINY).then_inc(const_made, 1)
            scale_q(0, 0, 48, None)
            for i in range(4):
                split(0, i, 0, None if i < 2 else i - 1)
            scale_q(1, 1, 48, None)
            for i in range(4):
                split(1, i, 1, 3 + i if i < 2 else unit(0, ("prep", i))[1] + 1)

            def body(hp):
                scale_q(hp * 2 + 2, 0, hp * 48 + 96, None)
                for i in range(4):
                    split(hp * 2 + 2, i, 0, unit(hp, ("prep", i + 4 if i < 2 else i + 8))[1] + 1)
                scale_q(hp * 2 + 3, 1, hp * 48 + 96, None)
                for i in range(4):
                    split(hp * 2 + 3, i, 1, (unit(hp, ("prep", i + 12)) if i < 2 else unit(hp + 1, ("prep", i)))[1] + 1)
            with pool.Fori(0, LOOPS) as hp:
                body(hp)

            pool.wait_ge(x_landed, 16)
            for c in range(NT // CT):
                pool.wait_ge(attn_made, (HEADS - 1) * (NB // 2) + c + 1)
                nc.gpsimd.tensor_tensor(attn[:, c * CT:(c + 1) * CT, :], attn[:, c * CT:(c + 1) * CT, :],
                                        x_raw[:, c * CT:(c + 1) * CT, :], ALU.add).then_inc(x_added, 1)
            pool.wait_ge(pv_done, STEPS * PVG)
            for hl in range(2):
                nc.gpsimd.tensor_copy(wn_hl[:, hl, :, D:D + 2],
                                      sum_cols[:, hl, :].rearrange("p (a b) -> p a b", a=1).broadcast_to([P, NT, 2]))\
                    .then_inc(sums_added, 1)
            for c in range(CHUNKS):
                for ot in range(KT):
                    pool.wait_ge(lo_taken, KT * c + ot + 1)
                    cols = slice(c * CC, (c + 1) * CC)
                    nc.gpsimd.tensor_tensor(prob[:, ot, cols], w_hl[:, 0, ot, cols].bitcast(F32),
                                            w_hl[:, 1, ot, cols].bitcast(F32), ALU.add).then_inc(wh_joined, 1)
                for t in range(c * CT, (c + 1) * CT):
                    block_ = mask[:, t, t * P:(t + 1) * P]
                    nc.gpsimd.affine_select(out=block_, in_=block_, compare_op=ALU.not_equal, fill=0.0, base=0,
                                            pattern=[[-1, P]], channel_multiplier=1).then_inc(diagonal_cleared, 1)

            def e_hi(b, t):
                if not exists1(b, t):
                    return
                pool.wait_ge(exped, b * NT + t + 1)
                if not isinstance(b, int) or b * NT + t >= ESLOTS:
                    pool.wait_ge(pv1_done, b * NT + t - ESLOTS + 1)
                stand(pool, pool_passed)
                nc.gpsimd.tensor_scalar(e_hl[:, 0, t % ESLOTS, :], slot1(t), 1.0, 0.0, ALU.mult, ALU.add)\
                    .then_inc(e_hi_made, 1)

            e_hi(0, 0)
            for t in range(4):
                e_hi(0, t + EXP_LEAD)
            with pool.Fori(0, CHUNKS - 1) as b:
                for t in range(4, NT + 4):
                    e_hi(b, t + EXP_LEAD)
            for t in range(4, NT):
                e_hi(CHUNKS - 1, t + EXP_LEAD)

        @block.tensor
        def _(pe):
            def take_unit(n):
                if isinstance(n, int) and n < 2:
                    return
                pe.wait_ge(unit_emptied, n - 1)

            def prep(i, slot, n, heads_before):
                take_unit(n)
                pe.wait_ge(parts_made, heads_before * 8 + (i * 2 + 2))
                for t in range(8):
                    mm = pe.transpose(score_ps[:, slot, t * P:(t + 1) * P],
                                      parts[i % 2][:, t, :, :].bitcast(F32).rearrange("p a b -> p (a b)"), ident[:])
                mm.then_inc(unit_filled, 1)

            def scores(s_static, c, slot, n, prep_units):
                b, t = (s_static // NB) % 2, (s_static % NB) * QT + c // NCH
                take_unit(n)
                if prep_units is not None:
                    pe.wait_ge(unit_emptied, prep_units)
                for i in range(CH // 512):
                    c0 = (c % NCH) * CH + i * 512
                    mm = pe.matmul(score_ps[:, slot, i * 512:(i + 1) * 512], q_hl[b][:, t * P:(t + 1) * P],
                                   k_hl[b][:, c0:c0 + 512], start=True, stop=True)
                mm.then_inc(unit_filled, 1)

            def turn(hp, k, u):
                s = hp * BODY + k
                pk, pu = (k, u - 3) if u >= 3 else (k - 1, (6, 7, 5)[u])
                if not (isinstance(s, int) and s == 0 and u < 3):
                    if not by_dve(pk, pu):
                        pe.wait_ge(act_copied, acts(hp, pk, pu))
                    else:
                        pe.wait_ge(dve_copied, dves(hp, pk, pu))
                elif u == 2:
                    pe.wait_ge(wt_copied, 1)
                if u == 0:
                    pe.wait_ge(tile_exped, s * QT + QT)
                for j in range(JU):
                    for i in range(QT):
                        mm = pe.transpose(turn_ps[u % 3][:, (j * QT + i) * P:(j * QT + i + 1) * P],
                                          prob[:, (k % 2) * QT + i, (u * JU + j) * P:(u * JU + j + 1) * P], ident[:])
                mm.then_inc(turned, 1)

            def finish(slot, n, pairs):
                take_unit(n)
                pe.wait_ge(o_taken, pairs)
                for i in range(2 * QT):
                    mm = pe.transpose(score_ps[:, slot, i * P:(i + 1) * P], o_part[:, i * P:(i + 1) * P], ident[:])
                mm.then_inc(unit_filled, 1)

            def step(hp, k):
                def live(j):
                    return not isinstance(hp, int) or hp * BODY + k + j < STEPS

                def T(u):
                    turn(hp, k, u)

                def V(g, back=0):
                    if g == 0 and k % 2 == 0:
                        pe.wait_ge(o_taken, hp * (BODY // 2) + k // 2)
                    pv_body(hp, k - back, g)

                def S(dk, c):
                    kk = k + dk
                    if live(dk):
                        need = unit(hp, ("prep", kk - NB + PREP_STEPS[-1]))[1] + 1 if kk % NB == 0 and c == 0 else None
                        scores(kk, c, *unit(hp, ("qk", kk, c)), need)

                def F():
                    if k % 2 == 0:
                        finish(*unit(hp, ("fin", k)), hp * (BODY // 2) + k // 2)

                def prepare():
                    if k % NB in PREP_STEPS and live(NB - k % NB):
                        heads = hp * 2 + (k // NB + 1)
                        prep(k % NB - PREP_STEPS[0], *unit(hp, ("prep", k)), heads)

                for op in PE_ORDER.split():
                    kind, args = op[0], [int(a) for a in op[1:]]
                    {"T": T, "V": V, "S": S, "F": F, "P": prepare}[kind](*args)

            def pv_body(hp, k, g):
                last = 2 * g + 1
                pe.wait_ge(act_copied, acts(hp, k, last))
                if any(by_dve(k, u) for u in range(last + 1)):
                    pe.wait_ge(dve_copied, dves(hp, k, last))
                b = (k // NB) % 2
                for q in range(4):
                    j = 4 * g + q
                    mm = pe.matmul(o_ps[HD * q:HD * q + HD, k % 2, :], raw[b][2][:, j, :],
                                   pt[:, j // JU, (j % JU) * QB:(j % JU + 1) * QB],
                                   start=(g == 0 and k % 2 == 0), stop=(g == PVG - 1), skip_group_check=True)
                mm.then_inc(pv_done, 1)

            pe.wait_ge(const_made, 6)
            for i in range(4):
                prep(i, i % 2, i, 0)
            pe.wait_ge(w_landed, 16)
            for it in range(KT):
                for ot in range(KT):
                    mm = pe.transpose(turn_ps[2][:, it * D + ot * P:it * D + (ot + 1) * P],
                                      w_raw[:, ot, it * P:(it + 1) * P], ident[:])
            mm.then_inc(wt_turned, 1)
            for c in range(SU):
                scores(0, c, c % 2, 4 + c, 4 if c == 0 else None)
            for c in range(2):
                scores(1, c, c % 2, 8 + c, None)
            for u in range(TU):
                turn(0, 0, u)
                if u == 3:
                    scores(1, 2, 0, 10, None)
                    pe.wait_ge(raw_in[0], 48)
                    pv_body(0, 0, 0)
                if u == 4:
                    scores(1, 3, 1, 11, None)
                if u == 5:
                    pv_body(0, 0, 1)
                if u == 6:
                    scores(2, 0, 0, 12, None)
            scores(2, 1, 1, 13, None)
            pv_body(0, 0, 2)
            with pe.Fori(0, LOOPS) as hp:
                for k in range(1, BODY + 1):
                    step(hp, k)
            for k in range(1, BODY):
                step(LOOPS, k)

            def seam_x(c):
                pe.wait_ge(x1_made, (c + 1) * CT)
                for kt in range(KT):
                    for t in range(CT):
                        mm = pe.transpose(score_ps[:, X_PAIR[c], kt * CC + t * P:kt * CC + (t + 1) * P],
                                          attn[:, c * CT + t, kt * P:(kt + 1) * P], ident[:])
                mm.then_inc(x1_turned, 1)

            def seam_w(c):
                pe.wait_ge(x1_copied, c + 1)
                for ot in range(KT):
                    i = KT * c + ot
                    if i >= len(wh_bank):
                        pe.wait_ge(lo_taken, i - len(wh_bank) + 1)
                    elif i == 0:
                        pe.wait_ge(act_copied, acts(LOOPS, BODY - 1, TU - 1))
                        pe.wait_ge(dve_copied, dves(LOOPS, BODY - 1, TU - 1))
                    elif i == len(wh_bank) - 1:
                        pe.wait_ge(o_taken, STEPS // 2)
                    for kt in range(KT):
                        mm = pe.matmul(wh_bank[i % len(wh_bank)], wt[:, kt, ot * P:(ot + 1) * P],
                                       prob[:, 2 + kt, c * CC:(c + 1) * CC], start=(kt == 0), stop=(kt == KT - 1))
                    mm.then_inc(wh_made, 1)

            def seam_v(c):
                pe.wait_ge(wh_joined, KT * (c + 1))
                if c < 2:
                    pe.wait_ge(x1_copied, 3 + c)
                else:
                    pe.wait_ge(lo_taken, KT * (c + 1))
                for h in range(2):
                    for i in range(2):
                        t = 2 * h + i
                        for ot in range(KT):
                            mm = pe.transpose(v_bank(c, h)[:, i, ot * P:(ot + 1) * P],
                                              prob[:, ot, c * CC + t * P:c * CC + (t + 1) * P], ident[:])
                    mm.then_inc(wh_turned, 1)

            def seam_m(c):
                pe.wait_ge(norm_made, c + 1)
                if c < 2:
                    pe.wait_ge(turned_lo, 2)
                else:
                    pe.wait_ge(norm_spread, c - 1)
                for t in range(CT):
                    mm = pe.transpose(m_bank(c)[:, t * P:(t + 1) * P],
                                      norm_col[:, c * CT + t:c * CT + t + 1].broadcast_to([P, P]), ident[:])
                mm.then_inc(norm_turned, 1)

            def seam(ops):
                for op in ops:
                    if op == "fin":
                        pv_body(LOOPS, BODY - 1, 3)
                        finish(FIN_SLOT, FIN_UNIT, STEPS // 2)
                        continue
                    kind, c = op[0], int(op[1])
                    if kind == "x":
                        if c < 2:
                            pe.wait_ge(unit_emptied, FIN_UNIT + c)
                        else:
                            pe.wait_ge(x1_copied, c - 1)
                    {"x": seam_x, "w": seam_w, "v": seam_v, "m": seam_m}[kind](c)

            seam(SEAM)

            def sims(b, t):
                if not exists1(b, t):
                    return
                n = b * NT + t
                if not isinstance(b, int) or n >= 4:
                    pe.wait_ge(sim_scaled, n - 3)
                elif n < 2:
                    pe.wait_ge(turned_lo, 4)
                    pe.wait_ge(diagonal_cleared, NT)
                else:
                    pe.wait_ge(norm_spread, n + 1)
                keys, blk = slice((t % NT) * P, (t % NT + 1) * P), b + t // NT
                terms = [(0, 0, 0), (0, 0, 1), (0, 1, 0), (0, 1, 1), (1, 0, 0), (1, 1, 0)]
                for m, (a, kt, q) in enumerate(terms):
                    pe.matmul(sim_bank(t), w_hl[:, a, kt, keys], w_hl[:, q, kt, bass.ds(blk * CC, CC)],
                              start=(m == 0), stop=False, skip_group_check=True)
                for i in range(CT):
                    mm = pe.matmul(sim_bank(t)[:, i * P:(i + 1) * P],
                                   mask[:, block_rows(blk, i), keys].rearrange("p a m -> p (a m)"), ident16[:],
                                   start=False, stop=True, skip_group_check=True)
                mm.then_inc(sim_filled, 1)

            def pv1(b, t):
                n, tk, blk = b * NT + t, t % NT, b + t // NT
                pe.wait_ge(e_hi_made, n + 1)
                pe.wait_ge(e_lo_made, n + 1)
                if isinstance(b, int) and n == 0:
                    pe.wait_ge(turned_lo, 2 * CHUNKS)
                    pe.wait_ge(sums_added, 2)
                for i in range(CT):
                    if tk == 0 and not (isinstance(b, int) and blk == 0):
                        pe.wait_ge(sums_taken, (blk - 1) * CT + (i + 1))
                    for m, (a, w) in enumerate(((0, 0), (0, 1), (1, 0))):
                        mm = pe.matmul(wh_bank[i][:, 0:D + 2], e_hl[:, a, t % ESLOTS, i * P:(i + 1) * P], wn_hl[:, w, tk, :],
                                       start=(tk == 0 and m == 0), stop=(tk == NT - 1 and m == 2), skip_group_check=True)
                mm.then_inc(pv1_done, 1)

            def step1(b, t):
                sims(b, t + SIM_LEAD)
                pv1(b, t)

            sims(0, 0)
            sims(0, 1)
            seam(SEAM_END)
            sims(0, 2)
            for t in range(4):
                step1(0, t)
            with pe.Fori(0, CHUNKS - 1) as b:
                for t in range(4, NT + 4):
                    step1(b, t)
            for t in range(4, NT):
                step1(CHUNKS - 1, t)

        @block.scalar
        def _(act):
            def exp_tile(n, kk, i):
                act.wait_ge(unit_emptied, n + 1)
                slot = (kk % 2) * QT + i
                r = (kk % 4) * QT + i
                nc.scalar.activation(prob[:, slot, :], prob[:, slot, :], ACT.Exp, bias=neg_max[:, r, 1:2], scale=-1.0,
                                     accum_out=row_sum[:, r:r + 1]).then_inc(tile_exped, 1)

            def copy(s, u, first=False):
                act.wait_ge(turned, s * TU + u + 1)
                if not first:
                    act.wait_ge(pv_done, (s - 1) * PVG + u // 2 + 1)
                nc.scalar.copy(pt[:, u, :], turn_ps[u % 3][:]).then_inc(act_copied, 1)

            def take_o(pairs):
                act.wait_ge(pv_done, pairs * (2 * PVG) + 2 * PVG)
                nc.scalar.copy(o_part[:], o_ps[:].rearrange("p a b -> p (a b)")).then_inc(o_taken, 1)

            def step(hp, k):
                s = hp * BODY + k
                more = not isinstance(s, int) or s + 1 < STEPS
                for op in ACT_ORDER.split():
                    kind, i = op[0], int(op[1])
                    if kind == "C" and not by_dve(k, i):
                        copy(s, i)
                    elif kind == "O" and k % 2 == 0:
                        take_o(hp * (BODY // 2) + (k // 2 - 1))
                    elif kind == "E" and more:
                        exp_tile(mask_unit(hp, k + 1, 2 * i + 1)[1], k + 1, i)

            def step0():
                for u in range(4):
                    if not by_dve(0, u):
                        copy(0, u, True)
                exp_tile(8 + 1, 1, 0)
                for u in range(4, TU):
                    if not by_dve(0, u):
                        copy(0, u, True)
                exp_tile(8 + 3, 1, 1)

            nc.scalar.preload_act_table_set("natural_log_exp_and_others")
            act.wait_ge(wt_turned, 1)
            nc.scalar.copy(wt[:].rearrange("p a b -> p (a b)"), turn_ps[2][:]).then_inc(wt_copied, 1)
            exp_tile(4 + 1, 0, 0)
            exp_tile(4 + 3, 0, 1)
            step0()
            with act.Fori(0, LOOPS) as hp:
                for k in range(1, BODY + 1):
                    step(hp, k)

            def root_var(c):
                act.wait_ge(aggregated, CT * (c + 1))
                if c == 0:
                    act.wait_ge(const_made, 6)
                nc.scalar.activation(rstd[:, c * CT:(c + 1) * CT], mean_var[:, c * CT:(c + 1) * CT, 1], ACT.Ln,
                                     bias=eps[:, 1:2]).then_inc(log_var, 1)
                act.wait_ge(log_var, c + 1)
                nc.scalar.activation(rstd[:, c * CT:(c + 1) * CT], rstd[:, c * CT:(c + 1) * CT], ACT.Exp,
                                     scale=-0.5).then_inc(rstd_made, 1)

            for k in range(1, BODY):
                step(LOOPS, k)
                if k in LN_STEPS[:-1]:
                    root_var(LN_STEPS.index(k))

            def copy_x1(c):
                act.wait_ge(x1_turned, c + 1)
                nc.scalar.copy(prob[:, 2:4, c * CC:(c + 1) * CC],
                               score_ps[:, X_PAIR[c], :].rearrange("p (a b) -> p a b", a=KT)).then_inc(x1_copied, 1)

            def take_hi(c):
                for ot in range(KT):
                    act.wait_ge(wh_made, KT * c + ot + 1)
                    nc.scalar.copy(w_hl[:, 0, ot, c * CC:(c + 1) * CC], wh_bank[(KT * c + ot) % len(wh_bank)]).then_inc(hi_taken, 1)

            def take_v(c):
                for h in range(2):
                    act.wait_ge(wh_turned, 2 * c + h + 1)
                    t0 = c * CT + 2 * h
                    nc.scalar.copy(wn_hl[:, 0, t0:t0 + 2, 0:D], v_bank(c, h)).then_inc(turned_hi, 1)
                    for i in range(2):
                        nc.scalar.activation(squares[:, 2 * h + i, :], v_bank(c, h)[:, i, :], ACT.Square,
                                             accum_out=norm_col[:, t0 + i:t0 + i + 1]).then_inc(squared, 1)
                act.wait_ge(squared, CT * (c + 1))
                cols = norm_col[:, c * CT:(c + 1) * CT]
                nc.scalar.activation(cols, cols, ACT.Ln, bias=eps[:, 2:3]).then_inc(log_square, 1)
                act.wait_ge(log_square, c + 1)
                nc.scalar.activation(cols, cols, ACT.Exp, scale=0.5).then_inc(norm_made, 1)

            copy_x1(0)
            take_o(STEPS // 2 - 1)
            root_var(CHUNKS - 2)
            take_hi(0)
            copy_x1(1)
            copy_x1(2)
            root_var(CHUNKS - 1)
            take_hi(1)
            copy_x1(3)
            take_hi(2)
            take_v(0)
            take_hi(3)
            take_v(1)
            take_v(2)

            def log_norms(b, t):
                if not exists1(b, t):
                    return
                n, tk = b * NT + t, t % NT
                if not isinstance(b, int) or n >= SLOTS1:
                    act.wait_ge(e_lo_made, n - SLOTS1 + 1)
                    stand(act, act_passed)
                elif n == 0:
                    act.wait_ge(norm_spread, 1)
                    act.wait_ge(wh_made, KT * CHUNKS)
                elif n == CT:
                    act.wait_ge(norm_spread, CHUNKS)
                nc.scalar.activation(slot1(t), norm_bc[:, bass.ds((b + t // NT) * CC, CC)], ACT.Ln, bias=eps[:, 0:1],
                                     scale=norm_col[:, tk:tk + 1]).then_inc(log_made, 1)

            def inv_norms(b, t):
                if exists1(b, t):
                    act.wait_ge(log_made, b * NT + t + 1)
                    nc.scalar.activation(slot1(t), slot1(t), ACT.Exp, scale=-1.0).then_inc(inv_norms_made, 1)

            def exp1(b, t):
                if exists1(b, t):
                    act.wait_ge(sim_scaled, b * NT + t + 1)
                    nc.scalar.activation(slot1(t), slot1(t), ACT.Exp).then_inc(exped, 1)

            def root1(b):
                act.wait_ge(var_made, (b + 1) * CT)
                nc.scalar.activation(rstd[:, 0:CT], mean_var[:, 0:CT, 1], ACT.Ln, bias=eps[:, 1:2]).then_inc(rstd1_log, 1)
                act.wait_ge(rstd1_log, b + 1)
                nc.scalar.activation(rstd[:, 0:CT], rstd[:, 0:CT], ACT.Exp, scale=-0.5).then_inc(rstd1_made, 1)

            def step1(b, t):
                log_norms(b, t + INV_LEAD)
                exp1(b, t + EXP_LEAD)
                inv_norms(b, t + INV_LEAD)
                if t == NT:
                    root1(b)

            for t in range(INV_LEAD):
                log_norms(0, t)
                inv_norms(0, t)
                if t == 1:
                    take_v(3)
            exp1(0, 0)
            for t in range(4):
                step1(0, t)
            with act.Fori(0, CHUNKS - 1) as b:
                for t in range(4, NT + 4):
                    step1(b, t)
            for t in range(4, NT):
                step1(CHUNKS - 1, t)
            root1(CHUNKS - 1)

        @block.vector
        def _(dve):
            def mask_scores(hp, kk, c, slot, n):
                i, h = c // NCH, c % NCH
                t = (kk % NB) * QT + i
                dve.wait_ge(unit_filled, n + 1)
                if c == 0 and not (isinstance(hp, int) and hp * BODY + kk < 2):
                    dve.wait_ge(turned, (hp * BODY + (kk - 1)) * TU)
                r = (kk % 4) * QT + i
                if h:
                    dve.wait_ge(unit_emptied, n)
                stand(dve, dve_passed)
                dve.wait_ge(mask_made, t + 1)
                nc.vector.tensor_tensor_reduce(
                    out=prob[:, (kk % 2) * QT + i, h * CH:(h + 1) * CH], in0=score_ps[:, slot, :],
                    in1=mask[:, t, h * CH:(h + 1) * CH], scale=-1.0,
                    scalar=3.0e38 if h == 0 else neg_max[:, r, 0:1],
                    op0=ALU.add, op1=ALU.min, accum_out=neg_max[:, r, h:h + 1]).then_inc(unit_emptied, 1)

            def make_mask(t):
                dve.wait_ge(adj_landed[t % 2], 16 * (t // 2 + 1))
                nc.vector.tensor_scalar(mask[:, t, :], adj_in[t % 2][:], 0.0, MASKED, ALU.is_le, ALU.mult)\
                    .then_inc(mask_made, 1)

            def prep(i, slot, n, b):
                dve.wait_ge(unit_filled, n + 1)
                dst = (q_hl if i < 2 else k_hl)[b]
                nc.vector.tensor_copy(dst[:, (i % 2) * CH:(i % 2 + 1) * CH], score_ps[:, slot, :])\
                    .then_inc(unit_emptied, 1)

            def copy(s, u, first):
                dve.wait_ge(turned, s * TU + u + 1)
                if not first:
                    dve.wait_ge(pv_done, (s - 1) * PVG + u // 2 + 1)
                nc.vector.tensor_copy(pt[:, u, :], turn_ps[u % 3][:]).then_inc(dve_copied, 1)

            def finish(hp, k, slot, n, pairs):
                r0 = ((k - 2) % 4) * QT
                nc.vector.reciprocal(inv_sum[:], row_sum[:, r0:r0 + 2 * QT]).then_inc(inv_made, 1)
                dve.wait_ge(unit_filled, n + 1)
                dve.wait_ge(inv_made, pairs + 1)
                t0 = ((k - 2) % NB) * QT
                cols = head_cols(hp, k - 2)
                nc.vector.tensor_reduce(o_sum[:], score_ps[:, slot, 0:512].rearrange("p (i g d) -> p i d g", g=4, d=HD),
                                        mybir.AxisListType.X, ALU.add).then_inc(unit_emptied, 1)
                dve.wait_ge(unit_emptied, n + 1)
                nc.vector.tensor_tensor(attn[:, t0:t0 + 2 * QT, cols], o_sum[:],
                                        inv_sum[:].rearrange("p (a b) -> p a b", b=1).broadcast_to([P, 2 * QT, HD]),
                                        ALU.mult).then_inc(attn_made, 1)

            def masks(hp, k, dk, c):
                kk = k + dk
                if isinstance(hp, int) and hp * BODY + kk >= STEPS:
                    return
                mask_scores(hp, kk, c, *mask_unit(hp, kk, c))

            def step(hp, k):
                if k + 1 < NB:
                    if isinstance(hp, int):
                        assert hp
                    else:
                        with dve.If(hp < 1):
                            for i in range(QT):
                                make_mask((k + 1) * QT + i)
                s = hp * BODY + k
                for op in DVE_ORDER.split():
                    kind, i = op[0], int(op[1])
                    if kind == "M":
                        masks(hp, k, 1, i)
                    elif kind == "F" and k % 2 == 0:
                        slot, n = unit(hp, ("fin", k))
                        finish(hp, k, slot, n, hp * (BODY // 2) + (k // 2 - 1))
                    elif kind == "P" and k % NB in PREP_STEPS and not (isinstance(hp, int) and s + NB - k % NB >= STEPS):
                        slot, n = unit(hp, ("prep", k))
                        prep(k % NB - PREP_STEPS[0], slot, n, (k // NB + 1) % 2)
                    elif kind == "C" and by_dve(k, i):
                        copy(s, i, False)

            prep(0, 0, 0, 0)
            make_mask(0)
            prep(1, 1, 1, 0)
            make_mask(1)
            prep(2, 0, 2, 0)
            prep(3, 1, 3, 0)
            for c in range(SU):
                mask_scores(0, 0, c, c % 2, 4 + c)
            for t in range(QT, 2 * QT):
                make_mask(t)
            for c in range(SU):
                mask_scores(0, 1, c, c % 2, 8 + c)
            for u in range(TU):
                if by_dve(0, u):
                    copy(0, u, True)
            with dve.Fori(0, LOOPS) as hp:
                for k in range(1, BODY + 1):
                    step(hp, k)

            def row_stats(c):
                dve.wait_ge(x_added, c + 1)
                if c:
                    dve.wait_ge(aggregated, CT * c)
                for t in range(CT):
                    nc.vector.bn_stats(stats[:, t, :], attn[:, c * CT + t, :]).then_inc(stats_made, 1)
                dve.wait_ge(stats_made, CT * (c + 1))
                for t in range(CT):
                    nc.vector.bn_aggr(mean_var[:, c * CT + t, :], stats[:, t, :]).then_inc(aggregated, 1)

            def normalise(c):
                dve.wait_ge(rstd_made, c + 1)
                for t in range(c * CT, (c + 1) * CT):
                    nc.vector.tensor_scalar(attn[:, t, :], attn[:, t, :], mean_var[:, t, 0:1], rstd[:, t:t + 1],
                                            ALU.subtract, ALU.mult).then_inc(x1_made, 1)

            for k in range(1, BODY):
                step(LOOPS, k)
                if k in LN_STEPS:
                    row_stats(LN_STEPS.index(k))
                if k - 1 in LN_STEPS and k - 1 != LN_STEPS[-1]:
                    normalise(LN_STEPS.index(k - 1))
            normalise(len(LN_STEPS) - 1)
            finish(LOOPS, BODY, FIN_SLOT, FIN_UNIT, STEPS // 2 - 1)

            def take_lo(c):
                for ot in range(KT):
                    dve.wait_ge(hi_taken, KT * c + ot + 1)
                    cols = slice(c * CC, (c + 1) * CC)
                    nc.vector.tensor_tensor(w_hl[:, 1, ot, cols], wh_bank[(KT * c + ot) % len(wh_bank)],
                                            w_hl[:, 0, ot, cols].bitcast(F32), ALU.subtract).then_inc(lo_taken, 1)

            def take_v(c):
                for h in range(2):
                    dve.wait_ge(squared, c * CT + 2 * h + 2)
                    dve.wait_ge(turned_hi, 2 * c + h + 1)
                    t0 = c * CT + 2 * h
                    nc.vector.tensor_tensor(wn_hl[:, 1, t0:t0 + 2, 0:D], v_bank(c, h),
                                            wn_hl[:, 0, t0:t0 + 2, 0:D].bitcast(F32), ALU.subtract).then_inc(turned_lo, 1)

            def spread_norm(c):
                dve.wait_ge(norm_turned, c + 1)
                nc.vector.tensor_copy(norm_bc[:, c * CC:(c + 1) * CC], m_bank(c)).then_inc(norm_spread, 1)

            take_lo(0)
            row_stats(CHUNKS - 1)
            normalise(CHUNKS - 1)
            take_lo(1)
            take_lo(2)
            take_v(0)
            take_lo(3)
            take_v(1)
            spread_norm(0)
            take_v(2)
            spread_norm(1)
            take_v(3)

            def scale(b, t):
                if not exists1(b, t):
                    return
                dve.wait_ge(inv_norms_made, b * NT + t + 1)
                dve.wait_ge(sim_filled, b * NT + t + 1)
                nc.vector.tensor_tensor(slot1(t), sim_bank(t), slot1(t), ALU.mult).then_inc(sim_scaled, 1)

            def e_lo(b, t):
                if not exists1(b, t):
                    return
                dve.wait_ge(e_hi_made, b * NT + t + 1)
                nc.vector.tensor_tensor(e_hl[:, 1, t % ESLOTS, :], slot1(t), e_hl[:, 0, t % ESLOTS, :].bitcast(F32),
                                        ALU.subtract).then_inc(e_lo_made, 1)

            def residual(b):
                dve.wait_ge(pv1_done, (b + 1) * NT)
                for i in range(CT):
                    nc.vector.reciprocal(inv_sum[:, i:i + 1], wh_bank[i][:, D:D + 1]).then_inc(inv1_made, 1)
                for i in range(CT):
                    row = attn[:, block_rows(b, i), :].rearrange("p a d -> p (a d)")
                    dve.wait_ge(inv1_made, b * CT + (i + 1))
                    nc.vector.scalar_tensor_tensor(out=row, in0=wh_bank[i][:, 0:D], scalar=inv_sum[:, i:i + 1], in1=row,
                                                   op0=ALU.mult, op1=ALU.add).then_inc(sums_taken, 1)
                dve.wait_ge(sums_taken, (b + 1) * CT)
                stand(dve, dve_passed)
                for i in range(CT):
                    nc.vector.bn_stats(stats[:, i, :], attn[:, block_rows(b, i), :].rearrange("p a d -> p (a d)"))\
                        .then_inc(y_made, 1)
                dve.wait_ge(y_made, (b + 1) * CT)
                stand(dve, dve_passed)
                for i in range(CT):
                    nc.vector.bn_aggr(mean_var[:, i, :], stats[:, i, :]).then_inc(var_made, 1)

            def normalise1(b):
                dve.wait_ge(rstd1_made, b + 1)
                for i in range(CT):
                    row = attn[:, block_rows(b, i), :].rearrange("p a d -> p (a d)")
                    nc.vector.tensor_scalar(row, row, mean_var[:, i, 0:1], rstd[:, i:i + 1],
                                            ALU.subtract, ALU.mult).then_inc(out_made, 1)

            def step1(b, t):
                scale(b, t + SCALE_LEAD)
                e_lo(b, t + EXP_LEAD)
                if t == NT - 1:
                    residual(b)
                if t == NT + 1:
                    normalise1(b)

            scale(0, 0)
            spread_norm(2)
            spread_norm(3)
            scale(0, 1)
            e_lo(0, 0)
            for t in range(4):
                step1(0, t)
            with dve.Fori(0, CHUNKS - 1) as b:
                for t in range(4, NT + 4):
                    step1(b, t)
            for t in range(4, NT):
                step1(CHUNKS - 1, t)
            normalise1(CHUNKS - 1)


def kernel(x, adj, L0_gnn_x2, L0_gnn_v, L1_gnn_W):
    import numpy as np
    import concourse.bacc as bacc
    from concourse.bass_utils import run_bass_kernel_spmd

    nc = bacc.Bacc("TRN2", target_bir_lowering=False, num_devices=1)
    arrays, args = {}, []
    for name, a in (("x", x), ("adj", adj), ("x2", L0_gnn_x2), ("v", L0_gnn_v), ("w", L1_gnn_W)):
        a = np.ascontiguousarray(a)
        arrays[f"in_{name}"] = a
        args.append(nc.dram_tensor(f"in_{name}", a.shape, mybir.dt.from_np(a.dtype), kind="ExternalInput").ap())
    args.append(nc.dram_tensor("out_0", x.shape, F32, kind="ExternalOutput").ap())
    build(nc, *args)
    r = run_bass_kernel_spmd(nc, [arrays], core_ids=[0])
    return r.results[0]["out_0"]
```
